# Optimizing a Trainium2 kernel written in Bass

```python
import numpy as np
import jax
import jax.numpy as jnp

def _softmax(x, axis=-1):
    return jax.nn.softmax(x, axis=axis)

def _gelu(x):
    return jax.nn.gelu(x, approximate=True)

def _silu(x):
    return jax.nn.silu(x)

def _sigmoid(x):
    return jax.nn.sigmoid(x)

def _layernorm(x, axis=-1, eps=1e-05):
    m = jnp.mean(x, axis=axis, keepdims=True)
    v = jnp.var(x, axis=axis, keepdims=True)
    return (x - m) / jnp.sqrt(v + eps)

def _scatter_add(tgt, idx, src, axis=0):
    return tgt.at[idx].add(src)

def _segment_sum(src, seg, n):
    return jax.ops.segment_sum(src, seg, n)
kernel_name = 'mk_audio_tower_d1_tok_aud1d512_r4_2ed2b3'

def setup_inputs(seed: int=0):
    np.random.seed(seed)
    _w = jnp.asarray

    def _rec_inputs():
        import jax
        import jax.numpy as jnp
        _rk = jax.random.key(seed)
        x = -0.00238186 + 1.00146 * jax.random.normal(jax.random.fold_in(_rk, 1), (64, 5000), jnp.float32)
        return x
    x = _rec_inputs()

    def _L0_tok_setup():
        import jax, jax.numpy as jnp
        import numpy as np
        B, E, G, P = (8, 16, 5000, 128)
        MASK_DENSITY = 0.1
        key = jax.random.key(seed)
        k_x, k_w, k_m = jax.random.split(key, 3)
        x = jax.random.normal(k_x, (B, G), dtype=jnp.float32)
        weight = jax.random.normal(k_w, (E, G, P), dtype=jnp.float32) * 0.01
        bias = jnp.zeros((E, P), dtype=jnp.float32)
        mask = (jax.random.uniform(k_m, (G, P)) < MASK_DENSITY).astype(jnp.float32)
        return {'x': x, 'weight': weight, 'bias': bias, 'mask': mask}
    _L0_tok_all = _L0_tok_setup()
    _L0_tok_in = {k: v for k, v in _L0_tok_all.items() if k in ('weight', 'bias', 'mask')}
    del _L0_tok_all

    def _L0_attn_setup():
        import jax, jax.numpy as jnp
        import numpy as np
        D_MODEL = 128
        N_HEADS = 8
        DH = D_MODEL // N_HEADS
        Q_PROJ = D_MODEL // 2
        KV_PROJ = 2 * D_MODEL // 3
        ROPE_DIM = D_MODEL // 8
        R = ROPE_DIM // N_HEADS
        THETA = 10000.0
        EPS = 1e-05
        B, S = (2, 512)

        def layernorm(x, g, b):
            m = jnp.mean(x, axis=-1, keepdims=True)
            v = jnp.var(x, axis=-1, keepdims=True)
            return (x - m) * jax.lax.rsqrt(v + EPS) * g + b

        def rope_cos_sin(seq_len, dtype):
            inv_freq = THETA ** (-jnp.arange(0, R, 2, dtype=jnp.float32) / R)
            ang = jnp.arange(seq_len, dtype=jnp.float32)[:, None] * inv_freq
            cos = jnp.concatenate([jnp.cos(ang), jnp.cos(ang)], axis=-1)
            sin = jnp.concatenate([jnp.sin(ang), jnp.sin(ang)], axis=-1)
            return (cos.astype(dtype), sin.astype(dtype))

        def apply_rope(x, cos, sin):
            x1, x2 = jnp.split(x, 2, axis=-1)
            rot = jnp.concatenate([-x2, x1], axis=-1)
            return x * cos + rot * sin

        def _reference_tuple_inner(x, W_dq, W_uq, W_qr, W_dkv, W_ukv, W_kr, W_o, q_ln_g, q_ln_b, kv_ln_g, kv_ln_b):
            b, s, d = x.shape
            cq = layernorm(x @ W_dq, q_ln_g, q_ln_b)
            Q = (cq @ W_uq).reshape(b, s, N_HEADS, DH).transpose(0, 2, 1, 3)
            Qr = (cq @ W_qr).reshape(b, s, N_HEADS, R).transpose(0, 2, 1, 3)
            cos, sin = rope_cos_sin(s, x.dtype)
            Qr = apply_rope(Qr, cos, sin)
            q = jnp.concatenate([Q, Qr], axis=-1)
            ckv = layernorm(x @ W_dkv, kv_ln_g, kv_ln_b)
            KV = ckv @ W_ukv
            K, V = (KV[..., :D_MODEL], KV[..., D_MODEL:])
            K = K.reshape(b, s, N_HEADS, DH).transpose(0, 2, 1, 3)
            Kr = (x @ W_kr).reshape(b, s, N_HEADS, R).transpose(0, 2, 1, 3)
            Kr = apply_rope(Kr, cos, sin)
            k = jnp.concatenate([K, Kr], axis=-1)
            v = V.reshape(b, s, N_HEADS, DH).transpose(0, 2, 1, 3)
            scale = 1.0 / jnp.sqrt(jnp.asarray(DH + R, x.dtype))
            scores = jnp.einsum('bhqd,bhkd->bhqk', q, k) * scale
            mask = jnp.tril(jnp.ones((s, s), dtype=bool))
            scores = jnp.where(mask, scores, jnp.finfo(scores.dtype).min)
            attn = jax.nn.softmax(scores, axis=-1)
            out = jnp.einsum('bhqk,bhkd->bhqd', attn, v)
            out = out.transpose(0, 2, 1, 3).reshape(b, s, d)
            return (out @ W_o.T, ckv)
        key = jax.random.key(seed)
        ks = jax.random.split(key, 9)
        p = lambda k, shape: 0.01 * jax.random.normal(k, shape, jnp.float32)
        return {'x': jax.random.normal(ks[0], (B, S, D_MODEL), jnp.float32), 'W_dq': p(ks[1], (D_MODEL, Q_PROJ)), 'W_uq': p(ks[2], (Q_PROJ, D_MODEL)), 'W_qr': p(ks[3], (Q_PROJ, ROPE_DIM)), 'W_dkv': p(ks[4], (D_MODEL, KV_PROJ)), 'W_ukv': p(ks[5], (KV_PROJ, 2 * D_MODEL)), 'W_kr': p(ks[6], (D_MODEL, ROPE_DIM)), 'W_o': p(ks[7], (D_MODEL, D_MODEL)), 'q_ln_g': jnp.ones((Q_PROJ,), jnp.float32), 'q_ln_b': jnp.zeros((Q_PROJ,), jnp.float32), 'kv_ln_g': jnp.ones((KV_PROJ,), jnp.float32), 'kv_ln_b': jnp.zeros((KV_PROJ,), jnp.float32)}
    _L0_attn_all = _L0_attn_setup()
    _L0_attn_in = {k: v for k, v in _L0_attn_all.items() if k in ('W_dq', 'W_uq', 'W_qr', 'W_dkv', 'W_ukv', 'W_kr', 'W_o', 'q_ln_g', 'q_ln_b', 'kv_ln_g', 'kv_ln_b')}
    del _L0_attn_all

    def _L0_ffn_setup():
        import jax, jax.numpy as jnp
        import numpy as np
        E = 64
        K = 2
        D = 128
        H = 64
        NSH = 2
        ROUTE_SCALE = 2.5
        CAP = 256
        STD = 0.02
        key = jax.random.key(seed)
        ks = jax.random.split(key, 8)
        x = jax.random.normal(ks[0], (4, 512, D), dtype=jnp.float32)
        gate_w = jax.random.normal(ks[1], (E, D), dtype=jnp.float32) * STD
        w1 = jax.random.normal(ks[2], (E, D, H), dtype=jnp.float32) * STD
        w3 = jax.random.normal(ks[3], (E, D, H), dtype=jnp.float32) * STD
        w2 = jax.random.normal(ks[4], (E, H, D), dtype=jnp.float32) * STD
        sw1 = jax.random.normal(ks[5], (D, H * NSH), dtype=jnp.float32) * STD
        sw3 = jax.random.normal(ks[6], (D, H * NSH), dtype=jnp.float32) * STD
        sw2 = jax.random.normal(ks[7], (H * NSH, D), dtype=jnp.float32) * STD
        return {'x': x, 'gate_w': gate_w, 'w1': w1, 'w3': w3, 'w2': w2, 'sw1': sw1, 'sw3': sw3, 'sw2': sw2}
    _L0_ffn_all = _L0_ffn_setup()
    _L0_ffn_in = {k: v for k, v in _L0_ffn_all.items() if k in ('gate_w', 'w1', 'w3', 'w2', 'sw1', 'sw3', 'sw2')}
    del _L0_ffn_all
    return {'x': x, 'L0_tok_weight': _L0_tok_in['weight'], 'L0_tok_bias': _L0_tok_in['bias'], 'L0_tok_mask': _L0_tok_in['mask'], 'L0_attn_W_dq': _L0_attn_in['W_dq'], 'L0_attn_W_uq': _L0_attn_in['W_uq'], 'L0_attn_W_qr': _L0_attn_in['W_qr'], 'L0_attn_W_dkv': _L0_attn_in['W_dkv'], 'L0_attn_W_ukv': _L0_attn_in['W_ukv'], 'L0_attn_W_kr': _L0_attn_in['W_kr'], 'L0_attn_W_o': _L0_attn_in['W_o'], 'L0_attn_q_ln_g': _L0_attn_in['q_ln_g'], 'L0_attn_q_ln_b': _L0_attn_in['q_ln_b'], 'L0_attn_kv_ln_g': _L0_attn_in['kv_ln_g'], 'L0_attn_kv_ln_b': _L0_attn_in['kv_ln_b'], 'L0_ffn_gate_w': _L0_ffn_in['gate_w'], 'L0_ffn_w1': _L0_ffn_in['w1'], 'L0_ffn_w3': _L0_ffn_in['w3'], 'L0_ffn_w2': _L0_ffn_in['w2'], 'L0_ffn_sw1': _L0_ffn_in['sw1'], 'L0_ffn_sw3': _L0_ffn_in['sw3'], 'L0_ffn_sw2': _L0_ffn_in['sw2']}

def reference(x, L0_tok_weight, L0_tok_bias, L0_tok_mask, L0_attn_W_dq, L0_attn_W_uq, L0_attn_W_qr, L0_attn_W_dkv, L0_attn_W_ukv, L0_attn_W_kr, L0_attn_W_o, L0_attn_q_ln_g, L0_attn_q_ln_b, L0_attn_kv_ln_g, L0_attn_kv_ln_b, L0_ffn_gate_w, L0_ffn_w1, L0_ffn_w3, L0_ffn_w2, L0_ffn_sw1, L0_ffn_sw3, L0_ffn_sw2):
    import jax
    import jax.numpy as jnp

    def _L0_tok_ref(x, weight, bias, mask):
        import jax, jax.numpy as jnp
        import numpy as np
        B, E, G, P = (8, 16, 5000, 128)
        MASK_DENSITY = 0.1
        W = weight * mask[None, :, :]
        out = jnp.einsum('bg,egp->bep', x, W)
        return out + bias[None, :, :]

    def _L0_attn_ref(x, W_dq, W_uq, W_qr, W_dkv, W_ukv, W_kr, W_o, q_ln_g, q_ln_b, kv_ln_g, kv_ln_b):
        import jax, jax.numpy as jnp
        import numpy as np
        D_MODEL = 128
        N_HEADS = 8
        DH = D_MODEL // N_HEADS
        Q_PROJ = D_MODEL // 2
        KV_PROJ = 2 * D_MODEL // 3
        ROPE_DIM = D_MODEL // 8
        R = ROPE_DIM // N_HEADS
        THETA = 10000.0
        EPS = 1e-05
        B, S = (2, 512)

        def layernorm(x, g, b):
            m = jnp.mean(x, axis=-1, keepdims=True)
            v = jnp.var(x, axis=-1, keepdims=True)
            return (x - m) * jax.lax.rsqrt(v + EPS) * g + b

        def rope_cos_sin(seq_len, dtype):
            inv_freq = THETA ** (-jnp.arange(0, R, 2, dtype=jnp.float32) / R)
            ang = jnp.arange(seq_len, dtype=jnp.float32)[:, None] * inv_freq
            cos = jnp.concatenate([jnp.cos(ang), jnp.cos(ang)], axis=-1)
            sin = jnp.concatenate([jnp.sin(ang), jnp.sin(ang)], axis=-1)
            return (cos.astype(dtype), sin.astype(dtype))

        def apply_rope(x, cos, sin):
            x1, x2 = jnp.split(x, 2, axis=-1)
            rot = jnp.concatenate([-x2, x1], axis=-1)
            return x * cos + rot * sin

        def _reference_tuple_inner(x, W_dq, W_uq, W_qr, W_dkv, W_ukv, W_kr, W_o, q_ln_g, q_ln_b, kv_ln_g, kv_ln_b):
            b, s, d = x.shape
            cq = layernorm(x @ W_dq, q_ln_g, q_ln_b)
            Q = (cq @ W_uq).reshape(b, s, N_HEADS, DH).transpose(0, 2, 1, 3)
            Qr = (cq @ W_qr).reshape(b, s, N_HEADS, R).transpose(0, 2, 1, 3)
            cos, sin = rope_cos_sin(s, x.dtype)
            Qr = apply_rope(Qr, cos, sin)
            q = jnp.concatenate([Q, Qr], axis=-1)
            ckv = layernorm(x @ W_dkv, kv_ln_g, kv_ln_b)
            KV = ckv @ W_ukv
            K, V = (KV[..., :D_MODEL], KV[..., D_MODEL:])
            K = K.reshape(b, s, N_HEADS, DH).transpose(0, 2, 1, 3)
            Kr = (x @ W_kr).reshape(b, s, N_HEADS, R).transpose(0, 2, 1, 3)
            Kr = apply_rope(Kr, cos, sin)
            k = jnp.concatenate([K, Kr], axis=-1)
            v = V.reshape(b, s, N_HEADS, DH).transpose(0, 2, 1, 3)
            scale = 1.0 / jnp.sqrt(jnp.asarray(DH + R, x.dtype))
            scores = jnp.einsum('bhqd,bhkd->bhqk', q, k) * scale
            mask = jnp.tril(jnp.ones((s, s), dtype=bool))
            scores = jnp.where(mask, scores, jnp.finfo(scores.dtype).min)
            attn = jax.nn.softmax(scores, axis=-1)
            out = jnp.einsum('bhqk,bhkd->bhqd', attn, v)
            out = out.transpose(0, 2, 1, 3).reshape(b, s, d)
            return (out @ W_o.T, ckv)
        return _reference_tuple_inner(x, W_dq, W_uq, W_qr, W_dkv, W_ukv, W_kr, W_o, q_ln_g, q_ln_b, kv_ln_g, kv_ln_b)[0]

    def _L0_ffn_ref(x, gate_w, w1, w3, w2, sw1, sw3, sw2):
        import jax, jax.numpy as jnp
        import numpy as np
        E = 64
        K = 2
        D = 128
        H = 64
        NSH = 2
        ROUTE_SCALE = 2.5
        CAP = 256
        STD = 0.02
        bs, slen, d = x.shape
        xf = x.reshape(-1, d)
        logits = xf @ gate_w.T
        scores = jax.nn.sigmoid(logits.astype(jnp.float32))
        top_scores, top_idx = jax.lax.top_k(scores, K)
        top_scores = top_scores / (top_scores.sum(-1, keepdims=True) + 1e-20)
        top_scores = top_scores * ROUTE_SCALE
        flat_e = top_idx.reshape(-1)
        x_pairs = jnp.repeat(xf, K, axis=0)
        oh = jax.nn.one_hot(flat_e, E, dtype=jnp.int32)
        pos = jnp.take_along_axis(jnp.cumsum(oh, axis=0), flat_e[:, None], axis=1)[:, 0] - 1
        buf = jnp.zeros((E, CAP, d), dtype=xf.dtype).at[flat_e, pos].set(x_pairs, mode='drop')
        h = jax.nn.silu(jnp.einsum('ecd,edh->ech', buf, w1)) * jnp.einsum('ecd,edh->ech', buf, w3)
        y = jnp.einsum('ech,ehd->ecd', h, w2)
        valid = (pos < CAP)[:, None]
        y_pairs = jnp.where(valid, y[flat_e, jnp.minimum(pos, CAP - 1)], 0.0)
        routed = (y_pairs.reshape(-1, K, d) * top_scores[..., None].astype(xf.dtype)).sum(axis=1)
        shared = jax.nn.silu(xf @ sw1) * (xf @ sw3) @ sw2
        return (shared + routed).reshape(bs, slen, d)
    h = _L0_tok_ref(x, L0_tok_weight, L0_tok_bias, L0_tok_mask)
    h = h + _L0_attn_ref(_layernorm(h, axis=-1), L0_attn_W_dq, L0_attn_W_uq, L0_attn_W_qr, L0_attn_W_dkv, L0_attn_W_ukv, L0_attn_W_kr, L0_attn_W_o, L0_attn_q_ln_g, L0_attn_q_ln_b, L0_attn_kv_ln_g, L0_attn_kv_ln_b)
    h = h + _L0_ffn_ref(_layernorm(h, axis=-1), L0_ffn_gate_w, L0_ffn_w1, L0_ffn_w3, L0_ffn_w2, L0_ffn_sw1, L0_ffn_sw3, L0_ffn_sw2)
    return h

_drawn_inputs = setup_inputs


def setup_inputs(seed=0):
    import zlib

    import numpy as np

    out = dict(_drawn_inputs(seed))
    spreads = {'L0_tok_bias': (0.0, 0.1),
     'L0_attn_q_ln_g': (1.0, 0.6),
     'L0_attn_q_ln_b': (0.0, 2.0),
     'L0_attn_kv_ln_g': (1.0, 0.6),
     'L0_attn_kv_ln_b': (0.0, 0.8)}
    factors = {'L0_attn_W_dq': 57.432,
     'L0_attn_W_uq': 200.0,
     'L0_attn_W_qr': 60.746,
     'L0_attn_W_kr': 61.065}
    for name, (base, spread) in spreads.items():
        noise = np.random.default_rng([zlib.crc32(name.encode()), seed]).standard_normal(out[name].shape)
        drawn = base * np.exp(spread * noise) if base else spread * noise
        out[name] = jnp.asarray(drawn.astype(out[name].dtype))
    for name, factor in factors.items():
        out[name] = (out[name] * factor).astype(out[name].dtype)
    return out
```

```python
import math
from contextlib import ExitStack

import numpy as np
import concourse.bass as bass
from concourse import mybir

ALU = mybir.AluOpType
ACT = mybir.ActivationFunctionType
AX = mybir.AxisListType
F32 = mybir.dt.float32
BF16 = mybir.dt.bfloat16
U32 = mybir.dt.uint32
I32 = mybir.dt.int32

P = 128
B, S, G, D = 64, 16, 5000, 128
NCH = 2 * B * (S // 2) // P
GC = G // P
GREM = G - GC * P
UC = GC // 3
UNITS = 6
RING = 2 * UNITS
NH, DH, R = 8, 16, 2
DK = DH + R
QP, KVP, RD = D // 2, 2 * D // 3, D // 8
E, H = 64, 64
SLOTS = 64
PAIRS = E // 2
PG = 4
GROUPS = PAIRS // PG
ROUTE_SCALE = 2.5
CAP = 256
POOL_UNIT = 4
EPS = 1e-5
NEG = -3.0e38
SCALE = 1.0 / math.sqrt(DK)
FAR = 100000.0

C_ID, C_IOTA, C_COS, C_SIN, C_W = 0, 128, 192, 208, 224
M_BEFORE, M_UPTO, M_SAME, M_W = 0, P, 2 * P, 3 * P


def shape_constants():
    c = np.zeros((P, C_W), np.float32)
    c[:, C_ID:C_ID + P] = np.eye(P)
    c[:, C_IOTA:C_IOTA + E] = np.arange(E)
    c[:, C_COS:C_COS + S] = np.cos(np.arange(S))
    c[:, C_SIN:C_SIN + S] = np.sin(np.arange(S))
    return c


def order_masks():
    half, batch = np.arange(P) // B, np.arange(P) % B
    m = np.zeros((P, M_W), np.float32)
    m[:, M_BEFORE:M_BEFORE + P] = batch[:, None] < batch[None, :]
    m[:, M_UPTO:M_UPTO + P] = batch[:, None] <= batch[None, :]
    m[:, M_SAME:M_SAME + P] = batch[:, None] * 2 + half[:, None] < batch[None, :] * 2 + half[None, :]
    return m


def tower_kernel(nc, x, tok_w, tok_b, tok_mask, W_dq, W_uq, W_qr, W_dkv, W_ukv, W_kr, W_o,
                 q_ln_g, q_ln_b, kv_ln_g, kv_ln_b, gate_w, w1, w3, w2, sw1, sw3, sw2, consts, masks, out):
    with ExitStack() as ctx:
        def sb(name, shape, dt=F32):
            return ctx.enter_context(nc.sbuf_tensor(name, shape, dt))

        def sem(name):
            return ctx.enter_context(nc.semaphore(name))

        xs_dram = nc.dram_tensor("expert_inputs", (E * SLOTS, D), F32, kind="Internal").ap()
        ys_dram = nc.dram_tensor("expert_outputs", (E * SLOTS, D), F32, kind="Internal").ap()

        bank = [ctx.enter_context(nc.psum_tensor(f"bank{i}", [P, 512], F32)) for i in range(8)]
        ring = sb("ring", [P, RING * UC * D])
        mask = sb("mask", [P, GC * D])
        w13 = sb("w13", [P, E, 2, H])
        w2p = sb("w2p", [P, PAIRS, D])
        xT = sb("xT", [P, GC * B])
        xrem = sb("xrem", [P, B])
        cst = sb("cst", [P, C_W])
        ltri = sb("ltri", [P, P], BF16)
        ones = sb("ones", [P, P], BF16)
        wproj = sb("wproj", [P, QP + KVP])
        wuq = sb("wuq", [P, D])
        wukv = sb("wukv", [P, 2 * D])
        lnp = sb("lnp", [P, 4])
        woT = sb("woT", [P, D])
        gwT = sb("gwT", [P, E])
        rope_in = sb("rope_in", [P, 2, RD])
        wkr = sb("wkr", [P, S, R, NH])
        wqr = sb("wqr", [P, S, R, NH])
        half = sb("half", [P, 2])
        hres = sb("hres", [P, NCH, D])
        xf = sb("xf", [P, NCH, D])
        xfT = sb("xfT", [P, NCH * P])
        xnT = sb("xnT", [P, P])
        oT = sb("oT", [P, P])
        stats = sb("stats", [P, 4, 6])
        mv = sb("mv", [P, 4, 2])
        rstd = sb("rstd", [P, 4])
        qkn = sb("qkn", [P, QP + KVP])
        cqT = sb("cqT", [P, P])
        ckvT = sb("ckvT", [P, P])
        kcat = sb("kcat", [P, S, NH, DK])
        vcat = sb("vcat", [P, S, D])
        qcat = sb("qcat", [P, NH, DK])
        prod = sb("prod", [P, S * NH * DK])
        sc = sb("sc", [P, 2, S * NH])
        mx = sb("mx", [P, 3, NH])
        o = sb("o", [P, 2, D])
        top = sb("top", [P, NCH, 8])
        topi = sb("topi", [P, NCH, 8], U32)
        ew = sb("ew", [P, 3, NCH, 2])
        wts = sb("wts", [P, NCH, 2])
        msel = sb("msel", [P, E], BF16)
        flag = sb("flag", [P, 2])
        flag_i = sb("flag_i", [P, 1], I32)
        msum = sb("msum", [P, NCH, E], BF16)
        rank = sb("rank", [P, 2])
        slot = sb("slot", [P, NCH, 2])
        far = sb("far", [P, 2])
        s_idx = sb("scatter_index", [P, NCH, 2], U32)
        g_idx = sb("gather_index", [P, NCH, 2], U32)

        wrem = w2p[0:GREM + 1, 0:S, :]

        def ring_view(a, n):
            return ring[:, a:a + n]
        xs = ring_view(0, PAIRS * D).rearrange("p (i d) -> p i d", d=D)
        ys = ring_view(4096, PAIRS * D).rearrange("p (i d) -> p i d", d=D)
        yg = ring_view(8192, 2 * NCH * D).rearrange("p (i d) -> p i d", d=D)
        xsT = [ring_view(10240 + 512 * i, 512) for i in range(2)]
        hT = [ring_view(11264 + 512 * i, 512) for i in range(2)]
        hm = [ring_view(12288 + 512 * i, 512).rearrange("p (i d) -> p i d", d=D) for i in range(2)]
        sil = [ring_view(13312 + 256 * i, 256).rearrange("p (i h) -> p i h", h=H) for i in range(2)]
        ssil = [ring_view(13824 + 512 * i, 512) for i in range(2)]
        shs = [ring_view(14848 + 512 * i, 512) for i in range(2)]
        fin = ring_view(15872, NCH * D).rearrange("p (j d) -> p j d", d=D)
        sw13 = ring_view(16896, 2 * D).rearrange("p (a d) -> p a d", a=2)
        sw2s = ring_view(17152, D)
        xst = w13[0:B].rearrange("p e a h -> p (e a h)")[:, 0:G]

        wo, gw, mrem = hres[:, NCH - 1, :], hres[:, NCH - 2, :], hres[:, NCH - 3, :]
        xn = qkn[:, 0:D]
        rjunk = prod[:, 0:2 * E].rearrange("p (k e) -> p k e", k=2)

        m_in = ring_view(0, M_W)
        m_bf = ring_view(512, M_W // 2).bitcast(BF16)
        sel_bf = ring_view(1024, NCH * E // 2).bitcast(BF16).rearrange("p (j e) -> p j e", e=E)
        pick = ring_view(1536, E)
        gates = ring_view(2048, NCH * E).rearrange("p (j e) -> p j e", e=E)
        f_sil = ring_view(3072, 2 * H).rearrange("p (a h) -> p a h", h=H)
        f_mid = ring_view(3328, 2 * H)
        f_midT = ring_view(3584, P)

        ident = cst[:, C_ID:C_ID + P]
        iota = cst[:, C_IOTA:C_IOTA + E]

        s_x, s_cst, s_rem, s_mrem = sem("x_in"), sem("cst_in"), sem("rem_in"), sem("mrem_in")
        s_pw, s_qw, s_tw, s_sw = sem("proj_w_in"), sem("qkv_w_in"), sem("turned_w_in"), sem("shared_w_in")
        s_mask = [sem(f"mask_in{t}") for t in range(3)]
        s_ring = [sem(f"ring_in{i}") for i in range(RING)]
        s_w13, s_w2 = sem("w13_in"), sem("w2_in")
        s_xs = [sem(f"xs_in{i}") for i in range(4)]
        s_ones, s_onesx, s_ltri, s_zsrc, s_zero = (sem("ones_set"), sem("ones_row_set"), sem("ltri_set"),
                                                   sem("zero_source"), sem("slots_zeroed"))
        s_xTp, s_xTs, s_wTp, s_wT, s_rope = (sem("x_transposed"), sem("xT_copied"), sem("w_transposed"),
                                             sem("wT_copied"), sem("rope_turned"))
        s_masked, s_pmask, s_remm, s_tok = sem("piece_masked"), sem("unit_masked_pool"), sem("rem_masked"), sem("third_summed")
        s_hres = sem("h_kept")
        s_var_h, s_var_qk, s_var_h2 = sem("variance_h"), sem("variance_qk"), sem("variance_h2")
        s_rstd_h, s_rstd_qk, s_rstd_h2 = sem("rstd_h"), sem("rstd_qk"), sem("rstd_h2")
        s_xn, s_xnT, s_xnTs, s_proj = sem("xn"), sem("xn_transposed"), sem("xnT_copied"), sem("projected")
        s_qkn, s_qkT, s_qkTs, s_qkv, s_kv = (sem("qk_normed"), sem("qk_transposed"), sem("qkT_copied"), sem("qkv"),
                                             sem("qkv_copied"))
        s_sc, s_p, s_o, s_oT, s_oTs, s_att = (sem("scores"), sem("probs"), sem("heads"), sem("o_transposed"),
                                              sem("oT_copied"), sem("attended"))
        s_xf, s_xfT, s_xfTs, s_gate = sem("xf"), sem("xf_transposed"), sem("xfT_copied"), sem("gate_logits")
        s_sel, s_count, s_rank, s_slot, s_scat = (sem("selected"), sem("counted_before"), sem("ranked"), sem("slots"),
                                                  sem("scattered"))
        s_top, s_exp, s_gidx = sem("top2"), sem("top2_exp"), sem("gather_slots")
        s_hmz = sem("mid_zeroed")
        s_sh1, s_ssil, s_shs, s_sh2, s_shared = (sem("shared_up"), sem("shared_silu"), sem("shared_mid"),
                                                 sem("shared_down"), sem("shared_added"))
        s_t1, s_xsT, s_m1, s_sil, s_hm, s_t2, s_hT, s_m2, s_ys = (
            sem("xs_transposed"), sem("xsT_copied"), sem("up"), sem("silu"), sem("mid"), sem("mid_transposed"),
            sem("midT_copied"), sem("down"), sem("y_copied"))
        s_yout = sem("y_out")
        s_yg = [sem(f"y_gathered{j}") for j in range(NCH)]
        s_fin, s_out = sem("final"), sem("out")
        s_total, s_flag = sem("expert_totals"), sem("flag")
        s_fm, s_fsel, s_fpos, s_fgate = sem("order_masks_in"), sem("full_selected"), sem("full_positions"), sem("full_gates")
        s_f1, s_fsil, s_fmid, s_ft, s_fT, s_f2, s_facc = (sem("full_up"), sem("full_silu"), sem("full_mid"),
            sem("full_transposed"), sem("full_midT"), sem("full_down"), sem("full_added"))
        s_fg = sem("full_product")
        s_dve, s_pool = sem("vector_chain"), sem("gpsimd_chain")

        tw = tok_w[:, 0:GC * P, :].rearrange("e (p c) n -> e p (c n)", c=GC)
        tm = tok_mask[0:GC * P, :].rearrange("(p c) n -> p (c n)", c=GC)

        def pool_masks(j, q):
            return q == POOL_UNIT and j < NCH - 1

        def pieces(j):
            return [(q, a, b) for q in range(UNITS) if not pool_masks(j, q) for a, b in ((0, 7), (7, UC))]

        def pieces_until(j, q):
            return sum(len(pieces(i)) for i in range(j)) + sum(u <= q for u, _, _ in pieces(j))

        def unit(j, q, a=0, b=UC):
            r = (j % 2) * UNITS + q
            return ring[:, (r * UC + a) * D:(r * UC + b) * D]

        block = ctx.enter_context(nc.Block())

        @block.sync
        def _(sp):
            for j in range(NCH):
                for q in range(UNITS):
                    t, par = q // 2, q % 2
                    if j == 0 and par == 0:
                        sp.dma_start(mask[:, t * UC * D:(t + 1) * UC * D],
                                     tm[:, t * UC * D:(t + 1) * UC * D]).then_inc(s_mask[t], 16)
                    if j >= 2:
                        sp.wait_ge(s_tok, 3 * (j - 2) + t + 1)
                    sp.dma_start(unit(j, q), tw[2 * j + par, :, t * UC * D:(t + 1) * UC * D]).then_inc(
                        s_ring[(j % 2) * UNITS + q], 16)
                    if j == 0 and q == 0:
                        sp.dma_start(xst, x).then_inc(s_x, 16)
                    if j == 0 and q == UNITS - 1:
                        sp.dma_start(wrem[0:GREM], tok_w[:, GC * P:G, :].rearrange("e g n -> g e n")).then_inc(s_rem, 16)
                        sp.dma_start(wrem[GREM:GREM + 1], tok_b.rearrange("(a e) n -> a e n", a=1)).then_inc(s_rem, 16)
                        sp.dma_start(mrem[0:GREM, :], tok_mask[GC * P:G, :]).then_inc(s_mrem, 16)
            sp.wait_ge(s_xTp, 5)
            sp.dma_start(w13[:, :, 0, :], w1.rearrange("e d h -> d e h")).then_inc(s_w13, 16)
            sp.dma_start(w13[:, :, 1, :], w3.rearrange("e d h -> d e h")).then_inc(s_w13, 16)
            sp.wait_ge(s_tok, 3 * NCH)
            sp.dma_start(sw13[:, 0, :], sw1).then_inc(s_sw, 16)
            sp.dma_start(sw13[:, 1, :], sw3).then_inc(s_sw, 16)
            sp.dma_start(sw2s, sw2).then_inc(s_sw, 16)
            for par in range(2):
                sp.dma_start(w2p[64 * par:64 * par + 64], w2[par::2].rearrange("i h d -> h i d")).then_inc(s_w2, 16)
            sp.wait_ge(s_scat, 16 * 2 * NCH)
            for i in range(4):
                sp.dma_start(xs[:, 8 * i:8 * i + 8, :],
                             xs_dram[1024 * i:1024 * (i + 1), :].rearrange("(i p) d -> p i d", p=P)).then_inc(s_xs[i], 16)
            for g in range(GROUPS):
                sp.wait_ge(s_ys, g + 1)
                sp.dma_start(ys_dram[512 * g:512 * (g + 1), :].rearrange("(i p) d -> p i d", p=P),
                             ys[:, PG * g:PG * g + PG, :]).then_inc(s_yout, 16)

            def write_out():
                for i in range(NCH // 2):
                    sp.wait_ge(s_fin, 2 * i + 2)
                    for par in range(2):
                        sp.dma_start(out[:, 4 * i + par:4 * i + 4:2, :],
                                     fin[64 * par:64 * par + 64, 2 * i:2 * i + 2, :]).then_inc(s_out, 16)

            write_out()
            sp.wait_ge(s_out, 16 * NCH)
            full = sp.value_load(flag_i[0:1, 0:1], min_val=0, max_val=1)
            with sp.If(full == 1):
                sp.wait_ge(s_yout, 16 * GROUPS)
                sp.dma_start(m_in, masks).then_inc(s_fm, 16)
                sp.wait_ge(s_facc, 1 + NCH * PAIRS)
                for par in range(2):
                    sp.dma_start(out[:, par::2, :], fin[64 * par:64 * par + 64]).then_inc(s_out, 16)
                sp.wait_ge(s_out, 16 * (NCH + 2))

        @block.gpsimd
        def _(pool):
            pool.memset(prod[:, 0:2048], 0.0).then_inc(s_zsrc, 1)
            pool.memset(half[:], -0.5).then_inc(s_pool, 1)
            pool.wait_ge(s_ones, 1)
            pool.affine_select(out=ltri[:], in_=ones[:], pattern=[[1, P]], compare_op=ALU.is_ge, fill=0.0,
                               base=-1, channel_multiplier=-1).then_inc(s_ltri, 1)
            pool.wait_ge(s_pool, 1)

            def root(s_var, n, a, b, s_rstd):
                pool.wait_ge(s_var, n)
                pool.tensor_tensor(rstd[:, a:b], mv[:, a:b, 1], half[:, 0:b - a], ALU.pow).then_inc(s_rstd, 1)

            def mask_unit(j):
                if j < NCH - 1:
                    q = POOL_UNIT
                    pool.wait_ge(s_ring[(j % 2) * UNITS + q], 16 * (j // 2 + 1))
                    if j == 0:
                        pool.wait_ge(s_mask[q // 2], 16)
                    pool.tensor_tensor(unit(j, q), unit(j, q), mask[:, (q // 2) * UC * D:(q // 2 + 1) * UC * D],
                                       ALU.mult).then_inc(s_pmask, 1)

            for c in range(NCH + 2):
                if 1 <= c <= NCH:
                    root(s_var_h, c, 0, 1, s_rstd_h)
                    root(s_var_qk, c, 1, 3, s_rstd_qk)
                if c >= 2:
                    root(s_var_h2, c - 1, 3, 4, s_rstd_h2)
                mask_unit(c)
                j = c - 2
                if j < 0:
                    continue
                if j == 0:
                    pool.wait_ge(s_zero, 32)
                pool.wait_ge(s_slot, j + 1)
                for k in range(2):
                    pool.indirect_dma_start(
                        out=xs_dram, out_offset=bass.IndirectOffsetOnAxis(ap=s_idx[:, j, k:k + 1], axis=0),
                        in_=xf[:, j, :], in_offset=None, bounds_check=E * SLOTS - 1, oob_is_err=False).then_inc(s_scat, 16)
            pool.wait_ge(s_gidx, 1)
            pool.wait_ge(s_yout, 16 * GROUPS)
            for j in range(NCH):
                for k in range(2):
                    pool.indirect_dma_start(
                        out=yg[:, 2 * j + k, :], out_offset=None, in_=ys_dram,
                        in_offset=bass.IndirectOffsetOnAxis(ap=g_idx[:, j, k:k + 1], axis=0),
                        bounds_check=E * SLOTS - 1, oob_is_err=False).then_inc(s_yg[j], 16)

        @block.scalar
        def _(act):
            act.dma_start(cst[:], consts).then_inc(s_cst, 16)
            act.dma_start(wproj[:, 0:QP], W_dq).then_inc(s_pw, 16)
            act.dma_start(wproj[:, QP:QP + KVP], W_dkv).then_inc(s_pw, 16)
            act.dma_start(rope_in[:, 0, :], W_kr).then_inc(s_pw, 16)
            act.dma_start(rope_in[0:QP, 1, :], W_qr).then_inc(s_pw, 16)
            act.dma_start(wuq[0:QP, :], W_uq).then_inc(s_qw, 16)
            act.dma_start(wukv[0:KVP, :], W_ukv).then_inc(s_qw, 16)
            for i, (v, n) in enumerate(((q_ln_g, QP), (q_ln_b, QP), (kv_ln_g, KVP), (kv_ln_b, KVP))):
                act.dma_start(lnp[0:n, i:i + 1], v.rearrange("(n a) -> n a", a=1)).then_inc(s_qw, 16)
            act.dma_start(wo, W_o).then_inc(s_tw, 16)
            act.dma_start(gw[0:E, :], gate_w).then_inc(s_tw, 16)
            act.wait_ge(s_zsrc, 1)
            for i in range(2):
                act.dma_start(xs_dram.rearrange("(p r) d -> p (r d)", p=P)[:, 2048 * i:2048 * (i + 1)],
                              prod[:, 0:2048]).then_inc(s_zero, 16)
            for i in range(5):
                act.wait_ge(s_xTp, i + 1)
                w = min(8, GC - 8 * i) * B
                act.copy(xT[:, 512 * i:512 * i + w], bank[i][:, 0:w]).then_inc(s_xTs, 1)
            act.wait_ge(s_onesx, 1)
            act.copy(xrem[0:GREM, :], bank[4][0:GREM, 448:512]).then_inc(s_xTs, 1)
            act.wait_ge(s_wTp, 1)
            act.copy(woT[:], bank[7][:, 0:D]).then_inc(s_wT, 1)
            act.copy(gwT[:], bank[7][:, D:D + E]).then_inc(s_wT, 1)

            def keep_h(j):
                act.wait_ge(s_tok, 3 * j + 3)
                act.copy(hres[:, j, :], bank[j % 2][:, 0:D]).then_inc(s_hres, 1)

            def copy_xnT(j):
                act.wait_ge(s_xnT, j + 1)
                act.copy(xnT[:], bank[2][:, 0:P]).then_inc(s_xnTs, 1)

            def copy_qkv(j):
                act.wait_ge(s_qkT, j + 1)
                act.activation(cqT[0:QP, :], bank[2][0:QP, 0:P], ACT.Identity, bias=lnp[0:QP, 1:2], scale=lnp[0:QP, 0:1])
                act.activation(ckvT[0:KVP, :], bank[2][0:KVP, P:2 * P], ACT.Identity,
                               bias=lnp[0:KVP, 3:4], scale=lnp[0:KVP, 2:3]).then_inc(s_qkTs, 1)
                act.copy(kcat[:, 2 * j:2 * j + 2, :, DH:DK].rearrange("p a h r -> p a r h"),
                         bank[5][:, 0:2 * RD].rearrange("p (a r h) -> p a r h", a=2, r=R))
                act.wait_ge(s_qkv, j + 1)
                act.copy(qcat[:, :, 0:DH], bank[3][:, 0:D].rearrange("p (h d) -> p h d", d=DH))
                act.copy(qcat[:, :, DH:DK].rearrange("p h r -> p r h"), bank[3][:, D:D + RD].rearrange("p (r h) -> p r h", r=R))
                act.copy(kcat[:, 2 * j:2 * j + 2, :, 0:DH],
                         bank[4][:].rearrange("p (a f) -> p a f", a=2)[:, :, 0:D].rearrange("p a (h d) -> p a h d", d=DH)
                         ).then_inc(s_kv, 1)
                act.copy(vcat[:, 2 * j:2 * j + 2, :],
                         bank[4][:].rearrange("p (a f) -> p a f", a=2)[:, :, D:2 * D]).then_inc(s_kv, 1)

            def probs(j):
                n = 2 * j + 2
                act.wait_ge(s_sc, j + 1)
                act.activation(sc[:, 0, 0:n * NH], sc[:, 1, 0:n * NH], ACT.Exp, scale=SCALE).then_inc(s_p, 1)

            def copy_oT(j):
                act.wait_ge(s_oT, j + 1)
                act.copy(oT[:], bank[6][:, 0:P]).then_inc(s_oTs, 1)

            def copy_xfT(j):
                act.wait_ge(s_xfT, j + 1)
                act.copy(xfT[:, P * j:P * j + P], bank[6][:, 256:384]).then_inc(s_xfTs, 1)

            act.wait_ge(s_qw, 16 * 6)
            for c in range(1, NCH + 2):
                if c <= NCH:
                    keep_h(c - 1)
                    copy_xnT(c - 1)
                if c >= 2:
                    probs(c - 2)
                    copy_oT(c - 2)
                if c <= NCH:
                    copy_qkv(c - 1)
                if c >= 2:
                    copy_xfT(c - 2)
            act.wait_ge(s_top, NCH)
            act.activation(ew[:, 0], top[:, :, 0:2], ACT.Exp, scale=-1.0).then_inc(s_exp, 1)

            for i in range(2):
                act.wait_ge(s_sh1, i + 1)
                act.activation(ssil[i], bank[2 + 2 * i][:], ACT.Silu).then_inc(s_ssil, 1)

            def silu(g):
                act.wait_ge(s_m1, g + 1)
                if g >= 2:
                    act.wait_ge(s_hm, g - 1)
                act.activation(sil[g % 2], bank[2 + g % 2][:].rearrange("p (i f) -> p i f", f=2 * H)[:, :, 0:H],
                               ACT.Silu).then_inc(s_sil, 1)

            def copy_midT(g):
                act.wait_ge(s_t2, g + 1)
                if g >= 2:
                    act.wait_ge(s_m2, g - 1)
                act.copy(hT[g % 2], bank[4 + g % 2][:]).then_inc(s_hT, 1)

            def copy_y(g):
                act.wait_ge(s_m2, g + 1)
                act.copy(ys[:, PG * g:PG * g + PG, :], bank[6 + g % 2][:].rearrange("p (i d) -> p i d", d=D)).then_inc(s_ys, 1)

            for g in range(GROUPS + 1):
                if g < GROUPS:
                    silu(g)
                if g >= 1:
                    copy_y(g - 1)
                if g < GROUPS:
                    copy_midT(g)

            act.wait_ge(s_flag, 1)
            full = act.value_load(flag_i[0:1, 0:1], min_val=0, max_val=1)
            with act.If(full == 1):
                with act.Fori(0, PAIRS) as i:
                    for j in range(NCH):
                        act.wait_ge(s_f1, i * NCH + (j + 1))
                        act.activation(f_sil, bank[0][:, 0:4 * H].rearrange("p (a f) -> p a f", a=2)[:, :, 0:H],
                                       ACT.Silu).then_inc(s_fsil, 1)
                        act.wait_ge(s_ft, i * NCH + (j + 1))
                        act.copy(f_midT, bank[1][:, 0:P]).then_inc(s_fT, 1)

        @block.tensor
        def _(pe):
            pe.wait_ge(s_cst, 16)
            pe.wait_ge(s_x, 16)
            for c in range(GC):
                last = pe.transpose(bank[c // 8][:, (c % 8) * B:(c % 8 + 1) * B], xst[:, c:GC * P:GC], ident[0:B, 0:B])
                if c % 8 == 7:
                    last.then_inc(s_xTp, 1)
            pe.transpose(bank[4][0:GREM, 448:512], xst[:, GC * P:G], ident[0:B, 0:B]).then_inc(s_xTp, 1)
            pe.wait_ge(s_tw, 32)
            pe.transpose(bank[7][:, 0:D], wo, ident)
            pe.transpose(bank[7][:, D:D + E], gw[0:E, :], ident[0:E, 0:E]).then_inc(s_wTp, 1)
            pe.wait_ge(s_xTs, 6)

            def sum_genes(j, t, a, b):
                for par in range(2):
                    q = 2 * t + par
                    if pool_masks(j, q):
                        pe.wait_ge(s_pmask, j + 1)
                    else:
                        pe.wait_ge(s_masked, pieces_until(j, q))
                if t == 0 and a == 0 and j >= 2:
                    pe.wait_ge(s_hres, j - 1)
                for c in range(a, b):
                    for par in range(2):
                        last = pe.matmul(bank[j % 2][64 * par:64 * par + 64, 0:D], xT[:, (UC * t + c) * B:(UC * t + c + 1) * B],
                                         unit(j, 2 * t + par, c, c + 1), start=(t == 0 and c == 0), stop=False)
                if t == 2:
                    if j == 0:
                        pe.wait_ge(s_remm, 1)
                        pe.wait_ge(s_rem, 32)
                    for par in range(2):
                        last = pe.matmul(bank[j % 2][64 * par:64 * par + 64, 0:D], xrem[0:GREM + 1, :],
                                         wrem[:, 2 * j + par, :], start=False, stop=True)
                if b == UC:
                    last.then_inc(s_tok, 1)

            def project(j):
                pe.wait_ge(s_xn, j + 1)
                pe.transpose(bank[2][:, 0:P], xn, ident).then_inc(s_xnT, 1)
                pe.wait_ge(s_xnTs, j + 1)
                if j >= 1:
                    pe.wait_ge(s_kv, 2 * j)
                pe.matmul(bank[3][:, 0:QP + KVP], xnT[:], wproj[:], start=True, stop=True).then_inc(s_proj, 1)
                for par in range(2):
                    for hf in range(2):
                        pe.matmul(bank[5][64 * hf:64 * hf + 64, RD * par:RD * par + RD], xnT[:, 64 * par:64 * par + 64],
                                  wkr[:, 2 * j + par].rearrange("p r h -> p (r h)"), start=True, stop=True)

            def qkv(j):
                pe.wait_ge(s_qkn, j + 1)
                pe.transpose(bank[2][0:QP, 0:P], qkn[:, 0:QP], ident)
                pe.transpose(bank[2][0:KVP, P:2 * P], qkn[:, QP:], ident).then_inc(s_qkT, 1)
                pe.wait_ge(s_qkTs, j + 1)
                for hf in range(2):
                    pe.matmul(bank[3][64 * hf:64 * hf + 64, D:D + RD], cqT[0:QP, 64 * hf:64 * hf + 64],
                              wqr[0:QP, 2 * j + hf].rearrange("p r h -> p (r h)"), start=True, stop=True)
                pe.matmul(bank[3][:, 0:D], cqT[0:QP, :], wuq[0:QP, :], start=True, stop=True)
                for par in range(2):
                    for hf in range(2):
                        last = pe.matmul(bank[4][64 * hf:64 * hf + 64, 256 * par:256 * par + 256],
                                         ckvT[0:KVP, 64 * par:64 * par + 64], wukv[0:KVP, :], start=True, stop=True)
                last.then_inc(s_qkv, 1)

            def attend(j):
                pe.wait_ge(s_o, j + 1)
                pe.transpose(bank[6][:, 0:P], o[:, 1, :], ident).then_inc(s_oT, 1)
                pe.wait_ge(s_oTs, j + 1)
                pe.matmul(bank[6][:, P:P + D], oT[:], woT[:], start=True, stop=True).then_inc(s_att, 1)

            def gate(j):
                pe.wait_ge(s_xf, j + 1)
                pe.transpose(bank[6][:, 256:384], xf[:, j, :], ident).then_inc(s_xfT, 1)
                pe.wait_ge(s_xfTs, j + 1)
                if j >= 1:
                    pe.wait_ge(s_slot, j)
                pe.matmul(bank[7][:, 0:E], xfT[:, P * j:P * j + P], gwT[:], start=True, stop=True).then_inc(s_gate, 1)

            def rank_tokens(j):
                pe.wait_ge(s_sel, j + 1)
                pe.wait_ge(s_top, j + 1)
                last = pe.matmul(bank[7][:, E:2 * E], ltri[:], msel[:], start=True, stop=(j == 0))
                if j >= 1:
                    pe.wait_ge(s_count, j)
                    last = pe.matmul(bank[7][:, E:2 * E], ones[:], msum[:, j - 1, :], start=False, stop=True)
                last.then_inc(s_rank, 1)

            for c in range(NCH + 2):
                if c == 1:
                    pe.wait_ge(s_wT, 2)
                    pe.wait_ge(s_ltri, 1)
                    pe.wait_ge(s_rope, 2)
                    pe.wait_ge(s_qw, 16 * 6)
                    pe.wait_ge(s_pw, 16 * 4)
                if 1 <= c <= NCH:
                    project(c - 1)
                if c >= 2:
                    attend(c - 2)
                if 1 <= c <= NCH:
                    qkv(c - 1)
                if c < NCH:
                    sum_genes(c, 0, 0, UC)
                if c >= 2:
                    gate(c - 2)
                if c < NCH:
                    sum_genes(c, 1, 0, 7)
                if c >= 2:
                    rank_tokens(c - 2)
                if c < NCH:
                    sum_genes(c, 1, 7, UC)
                    sum_genes(c, 2, 0, UC)

            pe.wait_ge(s_sw, 48)
            for i in range(2):
                for a in range(2):
                    last = pe.matmul(bank[2 + 2 * i + a][:], sw13[:, a, :], xfT[:, 512 * i:512 * i + 512], start=True, stop=True)
                last.then_inc(s_sh1, 1)
            pe.wait_ge(s_slot, NCH)
            pe.wait_ge(s_count, NCH)
            pe.matmul(bank[0][:, 0:E], ones[:], msum[:, NCH - 1, :], start=True, stop=True).then_inc(s_total, 1)
            for i in range(2):
                pe.wait_ge(s_shs, i + 1)
                for c in range(4):
                    last = pe.matmul(bank[6 + i][:, c * D:(c + 1) * D], shs[i][:, c * P:(c + 1) * P], sw2s,
                                     start=True, stop=True)
                last.then_inc(s_sh2, 1)

            def turn_xs(g):
                if g % 2 == 0:
                    pe.wait_ge(s_xs[g // 2], 16)
                if g == 0:
                    pe.wait_ge(s_flag, 1)
                if g >= 2:
                    pe.wait_ge(s_xsT, g - 1)
                for i in range(PG):
                    last = pe.transpose(bank[g % 2][:, i * P:(i + 1) * P], xs[:, PG * g + i, :], ident)
                last.then_inc(s_t1, 1)

            def up(g):
                pe.wait_ge(s_xsT, g + 1)
                if g == 0:
                    pe.wait_ge(s_w13, 32)
                    pe.wait_ge(s_shs, 2)
                if g >= 2:
                    pe.wait_ge(s_hm, g - 1)
                for i in range(PG):
                    for par in range(2):
                        last = pe.matmul(bank[2 + g % 2][64 * par:64 * par + 64, i * P:(i + 1) * P],
                                         xsT[g % 2][:, i * P + 64 * par:i * P + 64 * par + 64],
                                         w13[:, 2 * (PG * g + i) + par].rearrange("p a h -> p (a h)"),
                                         start=True, stop=True)
                last.then_inc(s_m1, 1)

            def turn_mid(g):
                pe.wait_ge(s_hm, g + 1)
                if g >= 2:
                    pe.wait_ge(s_hT, g - 1)
                for i in range(PG):
                    last = pe.transpose(bank[4 + g % 2][:, i * P:(i + 1) * P], hm[g % 2][:, i, :], ident)
                last.then_inc(s_t2, 1)

            def down(g):
                pe.wait_ge(s_hT, g + 1)
                if g == 0:
                    pe.wait_ge(s_w2, 32)
                    pe.wait_ge(s_shared, 2)
                if g >= 2:
                    pe.wait_ge(s_ys, g - 1)
                for i in range(PG):
                    last = pe.matmul(bank[6 + g % 2][:, i * D:(i + 1) * D], hT[g % 2][:, i * P:(i + 1) * P],
                                     w2p[:, PG * g + i, :], start=True, stop=True)
                last.then_inc(s_m2, 1)

            turn_xs(0)
            turn_xs(1)
            for g in range(GROUPS):
                up(g)
                if g >= 1:
                    down(g - 1)
                turn_mid(g)
                if g + 2 < GROUPS:
                    turn_xs(g + 2)
            down(GROUPS - 1)

            full = pe.value_load(flag_i[0:1, 0:1], min_val=0, max_val=1)
            with pe.If(full == 1):
                pe.wait_ge(s_fsel, NCH)
                pe.wait_ge(s_ys, GROUPS)
                for j in range(NCH):
                    if j >= 1:
                        pe.wait_ge(s_fgate, j)
                    for i in range(NCH):
                        m = M_UPTO if i < j else M_SAME if i == j else M_BEFORE
                        last = pe.matmul(bank[6][:, 0:E], m_bf[:, m:m + P], sel_bf[:, i, :], start=(i == 0), stop=(i == NCH - 1))
                    last.then_inc(s_fpos, 1)
                with pe.Fori(0, PAIRS) as i:
                    for j in range(NCH):
                        pe.wait_ge(s_facc, i * NCH + (j + 1))
                        pe.matmul(bank[0][:, 0:4 * H], xfT[:, P * j:P * j + P],
                                  w13[:].rearrange("p e a h -> p (e a h)")[:, bass.ds(i * (4 * H), 4 * H)],
                                  start=True, stop=True).then_inc(s_f1, 1)
                        pe.wait_ge(s_fmid, i * NCH + (j + 1))
                        pe.transpose(bank[1][:, 0:P], f_mid, ident).then_inc(s_ft, 1)
                        pe.wait_ge(s_fT, i * NCH + (j + 1))
                        pe.matmul(bank[2][:, 0:D], f_midT, w2p[:].rearrange("p i d -> p (i d)")[:, bass.ds(i * D, D)],
                                  start=True, stop=True).then_inc(s_f2, 1)

        @block.vector
        def _(dve):
            chain = [0]

            def mark(ins):
                chain[0] += 1
                ins.then_inc(s_dve, 1)

            def marked():
                dve.wait_ge(s_dve, chain[0])

            def then(ins):
                mark(ins)
                marked()

            dve.memset(ones[:], 1.0).then_inc(s_ones, 1)
            dve.memset(xrem[0:GREM + 1, :], 1.0).then_inc(s_onesx, 1)

            def turn_rope():
                dve.wait_ge(s_cst, 16)
                dve.wait_ge(s_pw, 64)
                for n, w, wr in ((P, wkr, 0), (QP, wqr, 1)):
                    win = rope_in[0:n, wr, :].rearrange("p (a h r) -> p a r h", a=1, r=R)
                    x1, x2 = (win[:, :, r, :].to_broadcast([n, S, NH]) for r in range(R))
                    cos, sin = (cst[0:n, c:c + S].rearrange("p (s a) -> p s a", a=1).to_broadcast([n, S, NH])
                                for c in (C_COS, C_SIN))
                    tmp = sc[0:n, 0, 0:S * NH].rearrange("p (s h) -> p s h", h=NH)
                    tmp2 = sc[0:n, 1, 0:S * NH].rearrange("p (s h) -> p s h", h=NH)
                    if wr:
                        dve.wait_ge(s_rope, 1)
                    mark(dve.tensor_tensor(w[0:n, :, 0, :], x1, cos, ALU.mult))
                    mark(dve.tensor_tensor(tmp, x2, sin, ALU.mult))
                    mark(dve.tensor_tensor(w[0:n, :, 1, :], x2, cos, ALU.mult))
                    mark(dve.tensor_tensor(tmp2, x1, sin, ALU.mult))
                    marked()
                    dve.tensor_tensor(w[0:n, :, 0, :], w[0:n, :, 0, :], tmp, ALU.subtract)
                    dve.tensor_tensor(w[0:n, :, 1, :], w[0:n, :, 1, :], tmp2, ALU.add).then_inc(s_rope, 1)

            def mask_piece(j, n):
                if j >= NCH or n >= len(pieces(j)):
                    return
                q, a, b = pieces(j)[n]
                dve.wait_ge(s_ring[(j % 2) * UNITS + q], 16 * (j // 2 + 1))
                if j == 0 and q % 2 == 0:
                    dve.wait_ge(s_mask[q // 2], 16)
                m = (q // 2) * UC
                dve.tensor_tensor(unit(j, q, a, b), unit(j, q, a, b), mask[:, (m + a) * D:(m + b) * D],
                                  ALU.mult).then_inc(s_masked, 1)

            def aggregate(a, b, s_var):
                for i in range(a, b):
                    mark(dve.bn_aggr(mv[:, i, :], stats[:, i, :]))
                marked()
                dve.tensor_scalar(mv[:, a:b, 1], mv[:, a:b, 1], EPS, None, ALU.add).then_inc(s_var, 1)

            def norm(out, v, i):
                return dve.tensor_scalar(out, v, mv[:, i, 0:1], rstd[:, i:i + 1], ALU.subtract, ALU.mult)

            def scores(j):
                n, f = 2 * j + 2, NH * DK
                dve.wait_ge(s_kv, 2 * j + 1)
                if j == 0:
                    dve.wait_ge(s_zero, 32)
                pr = prod[:, 0:n * f].rearrange("p (s f) -> p s f", f=f)
                then(dve.tensor_tensor(pr, kcat[:, 0:n].rearrange("p s h d -> p s (h d)"),
                                       qcat[:].rearrange("p (a h) d -> p a (h d)", a=1).to_broadcast([P, n, f]), ALU.mult))
                then(dve.tensor_reduce(sc[:, 0, 0:n * NH], prod[:, 0:n * f].rearrange("p (s d) -> p s d", d=DK), AX.X, ALU.add))
                then(dve.memset(sc[0:64, 0, (n - 1) * NH:n * NH], NEG))

            def less_max(j):
                n = 2 * j + 2
                sv = sc[:, 0, 0:n * NH].rearrange("p (s h) -> p s h", h=NH)
                then(dve.tensor_reduce(mx[:, 0, :], sv.rearrange("p s h -> p h s"), AX.X, ALU.max))
                dve.tensor_tensor(sc[:, 1, 0:n * NH].rearrange("p (s h) -> p s h", h=NH), sv,
                                  mx[:, 0:1, :].to_broadcast([P, n, NH]), ALU.subtract).then_inc(s_sc, 1)

            def heads(j):
                n = 2 * j + 2
                dve.wait_ge(s_p, j + 1)
                dve.wait_ge(s_kv, 2 * j + 2)
                pv = sc[:, 0, 0:n * NH].rearrange("p (s h) -> p s h", h=NH)
                mark(dve.tensor_reduce(mx[:, 1, :], pv.rearrange("p s h -> p h s"), AX.X, ALU.add))
                pr = prod[:, 0:n * D].rearrange("p (f d) -> p f d", d=DH)
                then(dve.tensor_tensor(pr, vcat[:, 0:n, :].rearrange("p s (h d) -> p (s h) d", d=DH),
                                       sc[:, 0, 0:n * NH].rearrange("p (f a) -> p f a", a=1).to_broadcast([P, n * NH, DH]), ALU.mult))
                mark(dve.reciprocal(mx[:, 2, :], mx[:, 1, :]))
                then(dve.tensor_reduce(o[:, 0, :], prod[:, 0:n * D].rearrange("p (s f) -> p f s", f=D), AX.X, ALU.add))
                dve.tensor_tensor(o[:, 1, :].rearrange("p (h d) -> p h d", d=DH), o[:, 0, :].rearrange("p (h d) -> p h d", d=DH),
                                  mx[:, 2, :].rearrange("p (h a) -> p h a", a=1).to_broadcast([P, NH, DH]), ALU.mult).then_inc(s_o, 1)

            def choose(j):
                dve.wait_ge(s_gate, j + 1)
                then(dve.max(top[:, j, :], bank[7][:, 0:E]))
                if j >= 1:
                    dve.wait_ge(s_rank, j)
                dve.tensor_scalar(msel[:], bank[7][:, 0:E], top[:, j, 1:2], None, ALU.is_ge).then_inc(s_sel, 1)
                dve.max_index(topi[:, j, :], top[:, j, :], bank[7][:, 0:E]).then_inc(s_top, 1)
                dve.wait_ge(s_sel, j + 1)
                if j >= 1:
                    dve.wait_ge(s_count, j)
                    dve.tensor_tensor(msum[:, j, :], msum[:, j - 1, :], msel[:], ALU.add).then_inc(s_count, 1)
                else:
                    dve.tensor_copy(msum[:, 0, :], msel[:]).then_inc(s_count, 1)

            def place(j):
                dve.wait_ge(s_rank, j + 1)
                dve.wait_ge(s_top, j + 1)
                for k in range(2):
                    mark(dve.scalar_tensor_tensor(rjunk[:, k], iota, topi[:, j, k:k + 1], bank[7][:, E:2 * E],
                                                  ALU.is_equal, ALU.mult, accum_out=rank[:, k:k + 1]))
                marked()
                mark(dve.scalar_tensor_tensor(slot[:, j, :], topi[:, j, 0:2], float(SLOTS), rank[:], ALU.mult, ALU.add))
                mark(dve.tensor_scalar(far[:], rank[:], float(SLOTS), FAR, ALU.is_ge, ALU.mult))
                marked()
                dve.tensor_tensor(s_idx[:, j, :], slot[:, j, :], far[:], ALU.add).then_inc(s_slot, 1)

            for c in range(NCH + 2):
                a, b = c - 1, c - 2
                project, attend = 0 <= a < NCH, b >= 0
                mask_piece(c, 0)
                if attend:
                    scores(b)
                if project:
                    dve.wait_ge(s_hres, a + 1)
                    then(dve.bn_stats(stats[:, 0, :], hres[:, a, :]))
                    aggregate(0, 1, s_var_h)
                mask_piece(c, 1)
                if project:
                    dve.wait_ge(s_rstd_h, a + 1)
                    norm(xn, hres[:, a, :], 0).then_inc(s_xn, 1)
                if attend:
                    less_max(b)
                mask_piece(c, 2)
                if c == 0:
                    turn_rope()
                if project:
                    dve.wait_ge(s_proj, a + 1)
                    mark(dve.bn_stats(stats[:, 1, :], bank[3][:, 0:QP]))
                    mark(dve.bn_stats(stats[:, 2, :], bank[3][:, QP:QP + KVP]))
                    marked()
                    aggregate(1, 3, s_var_qk)
                if attend:
                    heads(b)
                if project:
                    dve.wait_ge(s_rstd_qk, a + 1)
                    norm(qkn[:, 0:QP], bank[3][:, 0:QP], 1)
                    norm(qkn[:, QP:], bank[3][:, QP:QP + KVP], 2).then_inc(s_qkn, 1)
                mask_piece(c, 3)
                mask_piece(c, 4)
                if attend:
                    dve.wait_ge(s_att, b + 1)
                    then(dve.tensor_tensor(hres[:, b, :], hres[:, b, :], bank[6][:, P:P + D], ALU.add))
                    then(dve.bn_stats(stats[:, 3, :], hres[:, b, :]))
                    aggregate(3, 4, s_var_h2)
                mask_piece(c, 5)
                if attend:
                    dve.wait_ge(s_rstd_h2, b + 1)
                    norm(xf[:, b, :], hres[:, b, :], 3).then_inc(s_xf, 1)
                mask_piece(c, 6)
                mask_piece(c, 7)
                if attend:
                    choose(b)
                mask_piece(c, 8)
                if attend:
                    place(b)
                for n in range(9, 12):
                    mask_piece(c, n)
                if c == 0:
                    dve.wait_ge(s_rem, 32)
                    dve.wait_ge(s_mrem, 16)
                    dve.tensor_tensor(wrem[0:GREM], wrem[0:GREM],
                                      mrem[0:GREM, :].rearrange("p (a n) -> p a n", a=1).to_broadcast([GREM, S, D]),
                                      ALU.mult).then_inc(s_remm, 1)

            dve.tensor_scalar(g_idx[:], slot[:], float(E * SLOTS - 1), None, ALU.min).then_inc(s_gidx, 1)
            dve.wait_ge(s_tok, 3 * NCH)
            for i in range(2):
                dve.memset(hm[i], 0.0).then_inc(s_hmz, 1)
            dve.wait_ge(s_total, 1)
            then(dve.tensor_reduce(flag[:, 0:1], bank[0][:, 0:E], AX.X, ALU.max))
            dve.tensor_scalar(flag_i[:], flag[:, 0:1], float(SLOTS), None, ALU.is_gt).then_inc(s_flag, 1)
            for i in range(2):
                dve.wait_ge(s_ssil, i + 1)
                dve.tensor_tensor(shs[i], ssil[i], bank[3 + 2 * i][:], ALU.mult).then_inc(s_shs, 1)
            for i in range(2):
                dve.wait_ge(s_sh2, i + 1)
                hv = hres[:, 4 * i:4 * i + 4, :].rearrange("p j d -> p (j d)")
                dve.tensor_tensor(hv, hv, bank[6 + i][:], ALU.add).then_inc(s_shared, 1)
            dve.wait_ge(s_exp, 1)
            then(dve.tensor_scalar(ew[:, 1], ew[:, 0], 1.0, None, ALU.add))
            then(dve.reciprocal(ew[:, 2], ew[:, 1]))
            then(dve.scalar_tensor_tensor(ew[:, 0, :, 0], ew[:, 2, :, 0], 1e-20, ew[:, 2, :, 1], ALU.add, ALU.add))
            then(dve.reciprocal(ew[:, 0, :, 1], ew[:, 0, :, 0]))
            for k in range(2):
                mark(dve.scalar_tensor_tensor(wts[:, :, k], ew[:, 2, :, k], ROUTE_SCALE, ew[:, 0, :, 1], ALU.mult, ALU.mult))
            marked()

            def copy_xsT(g):
                dve.wait_ge(s_t1, g + 1)
                if g >= 2:
                    dve.wait_ge(s_m1, g - 1)
                dve.tensor_copy(xsT[g % 2], bank[g % 2][:]).then_inc(s_xsT, 1)

            def mid(g):
                dve.wait_ge(s_sil, g + 1)
                if g == 0:
                    dve.wait_ge(s_hmz, 2)
                if g >= 2:
                    dve.wait_ge(s_t2, g - 1)
                for par in range(2):
                    r = slice(64 * par, 64 * par + 64)
                    last = dve.tensor_tensor(hm[g % 2][r, :, 64 * par:64 * par + 64], sil[g % 2][r],
                                             bank[2 + g % 2][r].rearrange("p (i f) -> p i f", f=2 * H)[:, :, H:2 * H], ALU.mult)
                last.then_inc(s_hm, 1)

            copy_xsT(0)
            for g in range(GROUPS):
                if g + 1 < GROUPS:
                    copy_xsT(g + 1)
                mid(g)
            for j in range(NCH):
                dve.wait_ge(s_yg[j], 32)
                if j == 0:
                    dve.wait_ge(s_shared, 2)
                then(dve.scalar_tensor_tensor(fin[:, j, :], yg[:, 2 * j, :], wts[:, j, 0:1], hres[:, j, :], ALU.mult, ALU.add))
                dve.scalar_tensor_tensor(fin[:, j, :], yg[:, 2 * j + 1, :], wts[:, j, 1:2], fin[:, j, :],
                                         ALU.mult, ALU.add).then_inc(s_fin, 1)

            full = dve.value_load(flag_i[0:1, 0:1], min_val=0, max_val=1)
            with dve.If(full == 1):
                dve.wait_ge(s_fm, 16)
                mark(dve.tensor_copy(m_bf, m_in))
                for j in range(NCH):
                    then(dve.tensor_scalar(pick, iota, topi[:, j, 0:1], None, ALU.is_equal))
                    dve.scalar_tensor_tensor(sel_bf[:, j, :], iota, topi[:, j, 1:2], pick, ALU.is_equal, ALU.add).then_inc(s_fsel, 1)
                    dve.wait_ge(s_fsel, j + 1)
                for j in range(NCH):
                    if j >= 1:
                        dve.wait_ge(s_fgate, j)
                    then(dve.scalar_tensor_tensor(pick, iota, topi[:, j, 0:1], wts[:, j, 0:1].to_broadcast([P, E]),
                                                  ALU.is_equal, ALU.mult))
                    mark(dve.scalar_tensor_tensor(gates[:, j, :], iota, topi[:, j, 1:2], wts[:, j, 1:2].to_broadcast([P, E]),
                                                  ALU.is_equal, ALU.mult))
                    marked()
                    then(dve.tensor_tensor(pick, pick, gates[:, j, :], ALU.add))
                    dve.wait_ge(s_fpos, j + 1)
                    dve.scalar_tensor_tensor(gates[:, j, :], bank[6][:, 0:E], float(CAP), pick, ALU.is_lt, ALU.mult).then_inc(s_fgate, 1)
                dve.wait_ge(s_out, 16 * NCH)
                dve.wait_ge(s_fgate, NCH)
                dve.tensor_copy(fin[:], hres[:]).then_inc(s_facc, 1)
                with dve.Fori(0, PAIRS) as i:
                    for j in range(NCH):
                        dve.wait_ge(s_fsil, i * NCH + (j + 1))
                        dve.tensor_tensor(f_mid.rearrange("p (a h) -> p a h", h=H), f_sil,
                                          bank[0][:, 0:4 * H].rearrange("p (a f) -> p a f", a=2)[:, :, H:2 * H],
                                          ALU.mult).then_inc(s_fg, 1)
                        dve.wait_ge(s_fg, i * NCH + (j + 1))
                        gj = gates[:, j, bass.ds(i * 2, 2)].rearrange("p (a b) -> p a b", b=1)
                        dve.tensor_tensor(f_mid.rearrange("p (a h) -> p a h", h=H), f_mid.rearrange("p (a h) -> p a h", h=H),
                                          gj.to_broadcast([P, 2, H]), ALU.mult).then_inc(s_fmid, 1)
                        dve.wait_ge(s_f2, i * NCH + (j + 1))
                        dve.tensor_tensor(fin[:, j, :], fin[:, j, :], bank[2][:, 0:D], ALU.add).then_inc(s_facc, 1)


_INS = ['x', 'L0_tok_weight', 'L0_tok_bias', 'L0_tok_mask', 'L0_attn_W_dq', 'L0_attn_W_uq', 'L0_attn_W_qr', 'L0_attn_W_dkv',
        'L0_attn_W_ukv', 'L0_attn_W_kr', 'L0_attn_W_o', 'L0_attn_q_ln_g', 'L0_attn_q_ln_b', 'L0_attn_kv_ln_g',
        'L0_attn_kv_ln_b', 'L0_ffn_gate_w', 'L0_ffn_w1', 'L0_ffn_w3', 'L0_ffn_w2', 'L0_ffn_sw1', 'L0_ffn_sw3', 'L0_ffn_sw2']
_OUTS = [((B, S, D), 'float32')]


def kernel(**inputs):
    import numpy as _np
    import concourse.bacc as _bacc
    from concourse import mybir as _mybir
    from concourse.bass_utils import run_bass_kernel_spmd as _run

    nc = _bacc.Bacc("TRN2", target_bir_lowering=False, num_devices=1)
    arrays, args = {}, []
    for name in _INS:
        a = _np.ascontiguousarray(inputs[name])
        arrays[f"in_{name}_dram"] = a
        args.append(nc.dram_tensor(f"in_{name}_dram", a.shape, _mybir.dt.from_np(a.dtype), kind="ExternalInput").ap())
    for name, c in (("consts_dram", shape_constants()), ("masks_dram", order_masks())):
        arrays[name] = c
        args.append(nc.dram_tensor(name, c.shape, _mybir.dt.from_np(c.dtype), kind="ExternalInput").ap())
    for i, (shape, dtype) in enumerate(_OUTS):
        dt = _mybir.dt.from_np(_np.dtype(dtype))
        args.append(nc.dram_tensor(f"out_{i}_dram", shape, dt, kind="ExternalOutput").ap())
    tower_kernel(nc, *args)
    r = _run(nc, [arrays], core_ids=[0])
    got = tuple(r.results[0][f"out_{i}_dram"] for i in range(len(_OUTS)))
    return got[0]
```

```python
import math
from contextlib import ExitStack

from itertools import islice

import numpy as np
import concourse.bass as bass
from concourse import mybir

ALU = mybir.AluOpType
ACT = mybir.ActivationFunctionType
AX = mybir.AxisListType
F32 = mybir.dt.float32
BF16 = mybir.dt.bfloat16
U32 = mybir.dt.uint32
I32 = mybir.dt.int32

P = 128
B, S, G, D = 64, 16, 5000, 128
NCH = 2 * B * (S // 2) // P
GC = G // P
GREM = G - GC * P
UC = GC // 3
UNITS = 6
RING = 2 * UNITS
NH, DH, R = 8, 16, 2
DK = DH + R
QP, KVP, RD = D // 2, 2 * D // 3, D // 8
E, H = 64, 64
SLOTS = 64
PAIRS = E // 2
PG = 4
GROUPS = PAIRS // PG
ROUTE_SCALE = 2.5
CAP = 256
LEAD = 3
POOL_MORE = 3
HALVES = ((0, 7), (7, 13))
QUARTERS = ((0, 4), (4, 7), (7, 10), (10, 13))
EPS = 1e-5
NEG = -3.0e38
SCALE = 1.0 / math.sqrt(DK)
FAR = 100000.0

C_ID, C_IOTA, C_COS, C_SIN, C_W = 0, 128, 192, 208, 224
M_BEFORE, M_UPTO, M_SAME, M_W = 0, P, 2 * P, 3 * P


def shape_constants():
    c = np.zeros((P, C_W), np.float32)
    c[:, C_ID:C_ID + P] = np.eye(P)
    c[:, C_IOTA:C_IOTA + E] = np.arange(E)
    c[:, C_COS:C_COS + S] = np.cos(np.arange(S))
    c[:, C_SIN:C_SIN + S] = np.sin(np.arange(S))
    return c


def order_masks():
    half, batch = np.arange(P) // B, np.arange(P) % B
    m = np.zeros((P, M_W), np.float32)
    m[:, M_BEFORE:M_BEFORE + P] = batch[:, None] < batch[None, :]
    m[:, M_UPTO:M_UPTO + P] = batch[:, None] <= batch[None, :]
    m[:, M_SAME:M_SAME + P] = batch[:, None] * 2 + half[:, None] < batch[None, :] * 2 + half[None, :]
    return m


def tower_kernel(nc, x, tok_w, tok_b, tok_mask, W_dq, W_uq, W_qr, W_dkv, W_ukv, W_kr, W_o,
                 q_ln_g, q_ln_b, kv_ln_g, kv_ln_b, gate_w, w1, w3, w2, sw1, sw3, sw2, consts, masks, out):
    with ExitStack() as ctx:
        def sb(name, shape, dt=F32):
            return ctx.enter_context(nc.sbuf_tensor(name, shape, dt))

        def sem(name):
            return ctx.enter_context(nc.semaphore(name))

        xs_dram = nc.dram_tensor("expert_inputs", (E * SLOTS, D), F32, kind="Internal").ap()
        ys_dram = nc.dram_tensor("expert_outputs", (E * SLOTS, D), F32, kind="Internal").ap()

        bank = [ctx.enter_context(nc.psum_tensor(f"bank{i}", [P, 512], F32)) for i in range(8)]
        ring = sb("ring", [P, RING * UC * D])
        mask = sb("mask", [P, GC * D])
        w13 = sb("w13", [P, E, 2, H])
        w2p = sb("w2p", [P, PAIRS, D])
        xT = sb("xT", [P, GC * B])
        xrem = sb("xrem", [P, B])
        cst = sb("cst", [P, C_W])
        ltri = sb("ltri", [P, P], BF16)
        ones = sb("ones", [P, P], BF16)
        wproj = sb("wproj", [P, QP + KVP])
        wuq = sb("wuq", [P, D])
        wukv = sb("wukv", [P, 2 * D])
        lnp = sb("lnp", [P, 4])
        woT = sb("woT", [P, D])
        gwT = sb("gwT", [P, E])
        rope_in = sb("rope_in", [P, 2, RD])
        wkr = sb("wkr", [P, S, R, NH])
        wqr = sb("wqr", [P, S, R, NH])
        half = sb("half", [P, 2])
        hres = sb("hres", [P, NCH, D])
        xf = sb("xf", [P, NCH, D])
        xfT = sb("xfT", [P, NCH * P])
        xnT = sb("xnT", [P, P])
        oT = sb("oT", [P, P])
        stats = sb("stats", [P, 4, 6])
        mv = sb("mv", [P, 4, 2])
        rstd = sb("rstd", [P, 4])
        qkn = sb("qkn", [P, QP + KVP])
        cqT = sb("cqT", [P, P])
        ckvT = sb("ckvT", [P, P])
        kcat = sb("kcat", [P, S, NH, DK])
        vcat = sb("vcat", [P, S, D])
        qcat = sb("qcat", [P, NH, DK])
        prod = sb("prod", [P, S * NH * DK])
        sc = sb("sc", [P, 2, S * NH])
        mx = sb("mx", [P, 3, NH])
        o = sb("o", [P, 2, D])
        top = sb("top", [P, NCH, 8])
        topi = sb("topi", [P, NCH, 8], U32)
        ew = sb("ew", [P, 3, NCH, 2])
        wts = sb("wts", [P, NCH, 2])
        msel = sb("msel", [P, E], BF16)
        flag = sb("flag", [P, 2])
        flag_i = sb("flag_i", [P, 1], I32)
        msum = sb("msum", [P, NCH, E], BF16)
        rank = sb("rank", [P, 2])
        slot = sb("slot", [P, NCH, 2])
        far = sb("far", [P, 2])
        s_idx = sb("scatter_index", [P, NCH, 2], U32)
        g_idx = sb("gather_index", [P, NCH, 2], U32)

        wrem = w2p[0:GREM + 1, 0:S, :]

        def ring_view(a, n):
            return ring[:, a:a + n]
        xs = ring_view(0, PAIRS * D).rearrange("p (i d) -> p i d", d=D)
        ys = ring_view(4096, PAIRS * D).rearrange("p (i d) -> p i d", d=D)
        yg = ring_view(8192, 2 * NCH * D).rearrange("p (i d) -> p i d", d=D)
        xsT = [ring_view(10240 + 512 * i, 512) for i in range(2)]
        hT = [ring_view(11264 + 512 * i, 512) for i in range(2)]
        hm = [ring_view(12288 + 512 * i, 512).rearrange("p (i d) -> p i d", d=D) for i in range(2)]
        sil = [ring_view(13312 + 256 * i, 256).rearrange("p (i h) -> p i h", h=H) for i in range(2)]
        ssil = [ring_view(13824 + 512 * i, 512) for i in range(2)]
        shs = [ring_view(14848 + 512 * i, 512) for i in range(2)]
        fin = ring_view(15872, NCH * D).rearrange("p (j d) -> p j d", d=D)
        sw13 = ring_view(16896, 2 * D).rearrange("p (a d) -> p a d", a=2)
        sw2s = ring_view(17152, D)
        xst = w13[0:B].rearrange("p e a h -> p (e a h)")[:, 0:G]

        wo, gw, mrem = hres[:, NCH - 1, :], hres[:, NCH - 2, :], hres[:, NCH - 3, :]
        xn = qkn[:, 0:D]
        rjunk = prod[:, 0:2 * E].rearrange("p (k e) -> p k e", k=2)

        m_in = ring_view(0, M_W)
        m_bf = ring_view(512, M_W // 2).bitcast(BF16)
        sel_bf = ring_view(1024, NCH * E // 2).bitcast(BF16).rearrange("p (j e) -> p j e", e=E)
        pick = ring_view(1536, E)
        gates = ring_view(2048, NCH * E).rearrange("p (j e) -> p j e", e=E)
        f_sil = ring_view(3072, 2 * H).rearrange("p (a h) -> p a h", h=H)
        f_mid = ring_view(3328, 2 * H)
        f_midT = ring_view(3584, P)

        ident = cst[:, C_ID:C_ID + P]
        iota = cst[:, C_IOTA:C_IOTA + E]

        s_x, s_cst, s_rem, s_mrem = sem("x_in"), sem("cst_in"), sem("rem_in"), sem("mrem_in")
        s_pw, s_qw, s_tw, s_sw = sem("proj_w_in"), sem("qkv_w_in"), sem("turned_w_in"), sem("shared_w_in")
        s_mask = [sem(f"mask_in{t}") for t in range(3)]
        s_ring = [sem(f"ring_in{i}") for i in range(RING)]
        s_w13, s_w2 = sem("w13_in"), sem("w2_in")
        s_xs = [sem(f"xs_in{i}") for i in range(4)]
        s_ones, s_onesx, s_ltri, s_zsrc, s_zero = (sem("ones_set"), sem("ones_row_set"), sem("ltri_set"),
                                                   sem("zero_source"), sem("slots_zeroed"))
        s_xTp, s_xTs, s_wTp, s_wT, s_rope = (sem("x_transposed"), sem("xT_copied"), sem("w_transposed"),
                                             sem("wT_copied"), sem("rope_turned"))
        s_masked, s_pmask, s_remm, s_tok = sem("piece_masked"), sem("unit_masked_pool"), sem("rem_masked"), sem("third_summed")
        s_hres = sem("h_kept")
        s_var_h, s_var_qk, s_var_h2 = sem("variance_h"), sem("variance_qk"), sem("variance_h2")
        s_rstd_h, s_rstd_qk, s_rstd_h2 = sem("rstd_h"), sem("rstd_qk"), sem("rstd_h2")
        s_xn, s_xnT, s_xnTs, s_proj = sem("xn"), sem("xn_transposed"), sem("xnT_copied"), sem("projected")
        s_qkn, s_qkT, s_qkTs, s_qkv, s_kv = (sem("qk_normed"), sem("qk_transposed"), sem("qkT_copied"), sem("qkv"),
                                             sem("qkv_copied"))
        s_sc, s_p, s_o, s_oT, s_oTs, s_att = (sem("scores"), sem("probs"), sem("heads"), sem("o_transposed"),
                                              sem("oT_copied"), sem("attended"))
        s_xf, s_xfT, s_xfTs, s_gate = sem("xf"), sem("xf_transposed"), sem("xfT_copied"), sem("gate_logits")
        s_sel, s_count, s_rank, s_slot, s_scat = (sem("selected"), sem("counted_before"), sem("ranked"), sem("slots"),
                                                  sem("scattered"))
        s_top, s_exp, s_gidx = sem("top2"), sem("top2_exp"), sem("gather_slots")
        s_hmz = sem("mid_zeroed")
        s_sh1, s_ssil, s_shs, s_sh2, s_shared = (sem("shared_up"), sem("shared_silu"), sem("shared_mid"),
                                                 sem("shared_down"), sem("shared_added"))
        s_t1, s_xsT, s_m1, s_sil, s_hm, s_t2, s_hT, s_m2, s_ys = (
            sem("xs_transposed"), sem("xsT_copied"), sem("up"), sem("silu"), sem("mid"), sem("mid_transposed"),
            sem("midT_copied"), sem("down"), sem("y_copied"))
        s_yout = sem("y_out")
        s_yg = [sem(f"y_gathered{j}") for j in range(NCH)]
        s_fin, s_out = sem("final"), sem("out")
        s_total, s_flag = sem("expert_totals"), sem("flag")
        s_fm, s_fsel, s_fpos, s_fgate = sem("order_masks_in"), sem("full_selected"), sem("full_positions"), sem("full_gates")
        s_f1, s_fsil, s_fmid, s_ft, s_fT, s_f2, s_facc = (sem("full_up"), sem("full_silu"), sem("full_mid"),
            sem("full_transposed"), sem("full_midT"), sem("full_down"), sem("full_added"))
        s_fg = sem("full_product")
        s_dve, s_pool = sem("vector_chain"), sem("gpsimd_chain")

        tw = tok_w[:, 0:GC * P, :].rearrange("e (p c) n -> e p (c n)", c=GC)
        tm = tok_mask[0:GC * P, :].rearrange("(p c) n -> p (c n)", c=GC)

        def pool_units(j):
            return (2, 4) if POOL_MORE <= j < NCH - 1 else (4,)

        def halves(units):
            return [(q, a, b) for t in range(3) for a, b in HALVES for q in (2 * t, 2 * t + 1) if q in units]

        def vector_pieces(j):
            return halves([q for q in range(UNITS) if q not in pool_units(j)])

        def pool_pieces(j):
            return halves(pool_units(j))

        def masked_until(pieces, j, last):
            return sum(len(pieces(i)) for i in range(j)) + pieces(j).index(last) + 1

        def unit(j, q, a=0, b=UC):
            r = (j % 2) * UNITS + q
            return ring[:, (r * UC + a) * D:(r * UC + b) * D]

        block = ctx.enter_context(nc.Block())

        @block.sync
        def _(sp):
            for j in range(NCH):
                for q in range(UNITS):
                    t, par = q // 2, q % 2
                    if j == 0 and par == 0:
                        sp.dma_start(mask[:, t * UC * D:(t + 1) * UC * D],
                                     tm[:, t * UC * D:(t + 1) * UC * D]).then_inc(s_mask[t], 16)
                    if j >= 2:
                        sp.wait_ge(s_tok, 3 * (j - 2) + t + 1)
                    sp.dma_start(unit(j, q), tw[2 * j + par, :, t * UC * D:(t + 1) * UC * D]).then_inc(
                        s_ring[(j % 2) * UNITS + q], 16)
                    if j == 0 and q == 0:
                        sp.dma_start(xst, x).then_inc(s_x, 16)
                    if j == 0 and q == UNITS - 1:
                        sp.dma_start(wrem[0:GREM], tok_w[:, GC * P:G, :].rearrange("e g n -> g e n")).then_inc(s_rem, 16)
                        sp.dma_start(wrem[GREM:GREM + 1], tok_b.rearrange("(a e) n -> a e n", a=1)).then_inc(s_rem, 16)
                        sp.dma_start(mrem[0:GREM, :], tok_mask[GC * P:G, :]).then_inc(s_mrem, 16)
            sp.wait_ge(s_xTp, 5)
            sp.dma_start(w13[:, :, 0, :], w1.rearrange("e d h -> d e h")).then_inc(s_w13, 16)
            sp.dma_start(w13[:, :, 1, :], w3.rearrange("e d h -> d e h")).then_inc(s_w13, 16)
            sp.wait_ge(s_tok, 3 * NCH)
            sp.dma_start(sw13[:, 0, :], sw1).then_inc(s_sw, 16)
            sp.dma_start(sw13[:, 1, :], sw3).then_inc(s_sw, 16)
            sp.dma_start(sw2s, sw2).then_inc(s_sw, 16)
            for par in range(2):
                sp.dma_start(w2p[64 * par:64 * par + 64], w2[par::2].rearrange("i h d -> h i d")).then_inc(s_w2, 16)
            sp.wait_ge(s_scat, 16 * 2 * NCH)
            for i in range(4):
                sp.dma_start(xs[:, 8 * i:8 * i + 8, :],
                             xs_dram[1024 * i:1024 * (i + 1), :].rearrange("(i p) d -> p i d", p=P)).then_inc(s_xs[i], 16)
            for g in range(GROUPS):
                sp.wait_ge(s_ys, g + 1)
                sp.dma_start(ys_dram[512 * g:512 * (g + 1), :].rearrange("(i p) d -> p i d", p=P),
                             ys[:, PG * g:PG * g + PG, :]).then_inc(s_yout, 16)

            def write_out():
                for i in range(NCH // 2):
                    sp.wait_ge(s_fin, 2 * i + 2)
                    for par in range(2):
                        sp.dma_start(out[:, 4 * i + par:4 * i + 4:2, :],
                                     fin[64 * par:64 * par + 64, 2 * i:2 * i + 2, :]).then_inc(s_out, 16)

            write_out()
            sp.wait_ge(s_out, 16 * NCH)
            full = sp.value_load(flag_i[0:1, 0:1], min_val=0, max_val=1)
            with sp.If(full == 1):
                sp.wait_ge(s_yout, 16 * GROUPS)
                sp.dma_start(m_in, masks).then_inc(s_fm, 16)
                sp.wait_ge(s_facc, 1 + NCH * PAIRS)
                for par in range(2):
                    sp.dma_start(out[:, par::2, :], fin[64 * par:64 * par + 64]).then_inc(s_out, 16)
                sp.wait_ge(s_out, 16 * (NCH + 2))

        @block.gpsimd
        def _(pool):
            pool.memset(prod[:, 0:2048], 0.0).then_inc(s_zsrc, 1)
            pool.memset(half[:], -0.5).then_inc(s_pool, 1)
            pool.wait_ge(s_ones, 1)
            pool.affine_select(out=ltri[:], in_=ones[:], pattern=[[1, P]], compare_op=ALU.is_ge, fill=0.0,
                               base=-1, channel_multiplier=-1).then_inc(s_ltri, 1)
            pool.wait_ge(s_pool, 1)

            def root(s_var, n, a, b, s_rstd):
                pool.wait_ge(s_var, n)
                pool.tensor_tensor(rstd[:, a:b], mv[:, a:b, 1], half[:, 0:b - a], ALU.pow).then_inc(s_rstd, 1)

            def mask_piece(j, n):
                if j >= NCH or n >= len(pool_pieces(j)):
                    return
                q, a, b = pool_pieces(j)[n]
                pool.wait_ge(s_ring[(j % 2) * UNITS + q], 16 * (j // 2 + 1))
                if j == 0:
                    pool.wait_ge(s_mask[q // 2], 16)
                m = (q // 2) * UC
                pool.tensor_tensor(unit(j, q, a, b), unit(j, q, a, b), mask[:, (m + a) * D:(m + b) * D],
                                   ALU.mult).then_inc(s_pmask, 1)

            for c in range(NCH + 3):
                a, b, d = c - 1, c - 2, c - 3
                mask_piece(c, 0)
                if 0 <= d:
                    root(s_var_h2, d + 1, 3, 4, s_rstd_h2)
                if 0 <= b < NCH:
                    root(s_var_qk, b + 1, 1, 3, s_rstd_qk)
                mask_piece(c, 1)
                mask_piece(c, 2)
                if d >= 0:
                    if d == 0:
                        pool.wait_ge(s_zero, 32)
                    pool.wait_ge(s_slot, d + 1)
                    for k in range(2):
                        pool.indirect_dma_start(
                            out=xs_dram, out_offset=bass.IndirectOffsetOnAxis(ap=s_idx[:, d, k:k + 1], axis=0),
                            in_=xf[:, d, :], in_offset=None, bounds_check=E * SLOTS - 1, oob_is_err=False).then_inc(s_scat, 16)
                mask_piece(c, 3)
                if 0 <= a < NCH:
                    root(s_var_h, a + 1, 0, 1, s_rstd_h)
            pool.wait_ge(s_gidx, 1)
            pool.wait_ge(s_yout, 16 * GROUPS)
            for j in range(NCH):
                for k in range(2):
                    pool.indirect_dma_start(
                        out=yg[:, 2 * j + k, :], out_offset=None, in_=ys_dram,
                        in_offset=bass.IndirectOffsetOnAxis(ap=g_idx[:, j, k:k + 1], axis=0),
                        bounds_check=E * SLOTS - 1, oob_is_err=False).then_inc(s_yg[j], 16)

        @block.scalar
        def _(act):
            act.dma_start(cst[:], consts).then_inc(s_cst, 16)
            act.dma_start(wproj[:, 0:QP], W_dq).then_inc(s_pw, 16)
            act.dma_start(wproj[:, QP:QP + KVP], W_dkv).then_inc(s_pw, 16)
            act.dma_start(rope_in[:, 0, :], W_kr).then_inc(s_pw, 16)
            act.dma_start(rope_in[0:QP, 1, :], W_qr).then_inc(s_pw, 16)
            act.dma_start(wuq[0:QP, :], W_uq).then_inc(s_qw, 16)
            act.dma_start(wukv[0:KVP, :], W_ukv).then_inc(s_qw, 16)
            for i, (v, n) in enumerate(((q_ln_g, QP), (q_ln_b, QP), (kv_ln_g, KVP), (kv_ln_b, KVP))):
                act.dma_start(lnp[0:n, i:i + 1], v.rearrange("(n a) -> n a", a=1)).then_inc(s_qw, 16)
            act.dma_start(wo, W_o).then_inc(s_tw, 16)
            act.dma_start(gw[0:E, :], gate_w).then_inc(s_tw, 16)
            act.wait_ge(s_zsrc, 1)
            for i in range(2):
                act.dma_start(xs_dram.rearrange("(p r) d -> p (r d)", p=P)[:, 2048 * i:2048 * (i + 1)],
                              prod[:, 0:2048]).then_inc(s_zero, 16)
            for i in range(5):
                act.wait_ge(s_xTp, i + 1)
                w = min(8, GC - 8 * i) * B
                act.copy(xT[:, 512 * i:512 * i + w], bank[i][:, 0:w]).then_inc(s_xTs, 1)
            act.wait_ge(s_onesx, 1)
            act.copy(xrem[0:GREM, :], bank[4][0:GREM, 448:512]).then_inc(s_xTs, 1)
            def keep_h(j):
                act.wait_ge(s_tok, 3 * j + 3)
                act.copy(hres[:, j, :], bank[j % 2][:, 0:D]).then_inc(s_hres, 1)

            def copy_xnT(j):
                act.wait_ge(s_xnT, j + 1)
                act.copy(xnT[:], bank[2][:, 0:P]).then_inc(s_xnTs, 1)

            def copy_qkv(j):
                act.wait_ge(s_qkT, j + 1)
                act.activation(cqT[0:QP, :], bank[2][0:QP, 0:P], ACT.Identity, bias=lnp[0:QP, 1:2], scale=lnp[0:QP, 0:1])
                act.activation(ckvT[0:KVP, :], bank[2][0:KVP, P:2 * P], ACT.Identity,
                               bias=lnp[0:KVP, 3:4], scale=lnp[0:KVP, 2:3]).then_inc(s_qkTs, 1)
                act.copy(kcat[:, 2 * j:2 * j + 2, :, DH:DK].rearrange("p a h r -> p a r h"),
                         bank[5][:, 0:2 * RD].rearrange("p (a r h) -> p a r h", a=2, r=R))
                act.wait_ge(s_qkv, j + 1)
                act.copy(qcat[:, :, 0:DH], bank[3][:, 0:D].rearrange("p (h d) -> p h d", d=DH))
                act.copy(qcat[:, :, DH:DK].rearrange("p h r -> p r h"), bank[3][:, D:D + RD].rearrange("p (r h) -> p r h", r=R))
                act.copy(kcat[:, 2 * j:2 * j + 2, :, 0:DH],
                         bank[4][:].rearrange("p (a f) -> p a f", a=2)[:, :, 0:D].rearrange("p a (h d) -> p a h d", d=DH)
                         ).then_inc(s_kv, 1)
                act.copy(vcat[:, 2 * j:2 * j + 2, :],
                         bank[4][:].rearrange("p (a f) -> p a f", a=2)[:, :, D:2 * D]).then_inc(s_kv, 1)

            def probs(j):
                n = 2 * j + 2
                act.wait_ge(s_sc, j + 1)
                act.activation(sc[:, 0, 0:n * NH], sc[:, 1, 0:n * NH], ACT.Exp, scale=SCALE).then_inc(s_p, 1)

            def copy_oT(j):
                act.wait_ge(s_oT, j + 1)
                act.copy(oT[:], bank[6][:, 0:P]).then_inc(s_oTs, 1)

            def copy_xfT(j):
                act.wait_ge(s_xfT, j + 1)
                act.copy(xfT[:, P * j:P * j + P], bank[6][:, 256:384]).then_inc(s_xfTs, 1)

            act.wait_ge(s_qw, 16 * 6)
            for c in range(NCH + 3):
                a, b, d = c - 1, c - 2, c - 3
                if c == 1:
                    act.wait_ge(s_wTp, 1)
                    act.copy(woT[:], bank[7][:, 0:D]).then_inc(s_wT, 1)
                    act.copy(gwT[:], bank[7][:, D:D + E]).then_inc(s_wT, 1)
                if 0 <= d:
                    copy_oT(d)
                if 0 <= b < NCH:
                    copy_xnT(b)
                if 0 <= d:
                    copy_xfT(d)
                if 0 <= b < NCH:
                    copy_qkv(b)
                if 0 <= a < NCH:
                    keep_h(a)
                if 0 <= b < NCH:
                    probs(b)
            act.wait_ge(s_top, NCH)
            act.activation(ew[:, 0], top[:, :, 0:2], ACT.Exp, scale=-1.0).then_inc(s_exp, 1)

            for i in range(2):
                act.wait_ge(s_sh1, i + 1)
                act.activation(ssil[i], bank[2 + 2 * i][:], ACT.Silu).then_inc(s_ssil, 1)

            def silu(g):
                act.wait_ge(s_m1, g + 1)
                if g >= 2:
                    act.wait_ge(s_hm, g - 1)
                act.activation(sil[g % 2], bank[2 + g % 2][:].rearrange("p (i f) -> p i f", f=2 * H)[:, :, 0:H],
                               ACT.Silu).then_inc(s_sil, 1)

            def copy_midT(g):
                act.wait_ge(s_t2, g + 1)
                if g >= 2:
                    act.wait_ge(s_m2, g - 1)
                act.copy(hT[g % 2], bank[4 + g % 2][:]).then_inc(s_hT, 1)

            def copy_y(g):
                act.wait_ge(s_m2, g + 1)
                act.copy(ys[:, PG * g:PG * g + PG, :], bank[6 + g % 2][:].rearrange("p (i d) -> p i d", d=D)).then_inc(s_ys, 1)

            for g in range(GROUPS + 1):
                if g < GROUPS:
                    silu(g)
                if g >= 1:
                    copy_y(g - 1)
                if g < GROUPS:
                    copy_midT(g)

            act.wait_ge(s_flag, 1)
            full = act.value_load(flag_i[0:1, 0:1], min_val=0, max_val=1)
            with act.If(full == 1):
                with act.Fori(0, PAIRS) as i:
                    for j in range(NCH):
                        act.wait_ge(s_f1, i * NCH + (j + 1))
                        act.activation(f_sil, bank[0][:, 0:4 * H].rearrange("p (a f) -> p a f", a=2)[:, :, 0:H],
                                       ACT.Silu).then_inc(s_fsil, 1)
                        act.wait_ge(s_ft, i * NCH + (j + 1))
                        act.copy(f_midT, bank[1][:, 0:P]).then_inc(s_fT, 1)

        @block.tensor
        def _(pe):
            pe.wait_ge(s_cst, 16)
            pe.wait_ge(s_x, 16)
            for c in range(GC):
                last = pe.transpose(bank[c // 8][:, (c % 8) * B:(c % 8 + 1) * B], xst[:, c:GC * P:GC], ident[0:B, 0:B])
                if c % 8 == 7:
                    last.then_inc(s_xTp, 1)
            pe.transpose(bank[4][0:GREM, 448:512], xst[:, GC * P:G], ident[0:B, 0:B]).then_inc(s_xTp, 1)
            pe.wait_ge(s_xTs, 6)

            def sum_genes(j, n):
                if j >= NCH:
                    return
                t, (a, b) = n // 4, QUARTERS[n % 4]
                half = next(h for h in HALVES if b <= h[1])
                for q in (2 * t, 2 * t + 1):
                    s_done, pieces = (s_pmask, pool_pieces) if q in pool_units(j) else (s_masked, vector_pieces)
                    pe.wait_ge(s_done, masked_until(pieces, j, (q, *half)))
                if t == 0 and a == 0 and j >= 2:
                    pe.wait_ge(s_hres, j - 1)
                for c in range(a, b):
                    for par in range(2):
                        last = pe.matmul(bank[j % 2][64 * par:64 * par + 64, 0:D], xT[:, (UC * t + c) * B:(UC * t + c + 1) * B],
                                         unit(j, 2 * t + par, c, c + 1), start=(t == 0 and c == 0), stop=False)
                if n == 11:
                    if j == 0:
                        pe.wait_ge(s_remm, 1)
                        pe.wait_ge(s_rem, 32)
                    for par in range(2):
                        last = pe.matmul(bank[j % 2][64 * par:64 * par + 64, 0:D], xrem[0:GREM + 1, :],
                                         wrem[:, 2 * j + par, :], start=False, stop=True)
                if n % 4 == 3:
                    last.then_inc(s_tok, 1)

            def turn_xn(j):
                pe.wait_ge(s_xn, j + 1)
                pe.transpose(bank[2][:, 0:P], xn, ident).then_inc(s_xnT, 1)

            def project(j):
                pe.wait_ge(s_xnTs, j + 1)
                if j >= 1:
                    pe.wait_ge(s_kv, 2 * j)
                pe.matmul(bank[3][:, 0:QP + KVP], xnT[:], wproj[:], start=True, stop=True).then_inc(s_proj, 1)
                for par in range(2):
                    for hf in range(2):
                        pe.matmul(bank[5][64 * hf:64 * hf + 64, RD * par:RD * par + RD], xnT[:, 64 * par:64 * par + 64],
                                  wkr[:, 2 * j + par].rearrange("p r h -> p (r h)"), start=True, stop=True)

            def turn_qk(j):
                pe.wait_ge(s_qkn, j + 1)
                pe.transpose(bank[2][0:QP, 0:P], qkn[:, 0:QP], ident)
                pe.transpose(bank[2][0:KVP, P:2 * P], qkn[:, QP:], ident).then_inc(s_qkT, 1)

            def qkv(j):
                pe.wait_ge(s_qkTs, j + 1)
                for hf in range(2):
                    pe.matmul(bank[3][64 * hf:64 * hf + 64, D:D + RD], cqT[0:QP, 64 * hf:64 * hf + 64],
                              wqr[0:QP, 2 * j + hf].rearrange("p r h -> p (r h)"), start=True, stop=True)
                pe.matmul(bank[3][:, 0:D], cqT[0:QP, :], wuq[0:QP, :], start=True, stop=True)
                for par in range(2):
                    for hf in range(2):
                        last = pe.matmul(bank[4][64 * hf:64 * hf + 64, 256 * par:256 * par + 256],
                                         ckvT[0:KVP, 64 * par:64 * par + 64], wukv[0:KVP, :], start=True, stop=True)
                last.then_inc(s_qkv, 1)

            def turn_o(j):
                pe.wait_ge(s_o, j + 1)
                pe.transpose(bank[6][:, 0:P], o[:, 1, :], ident).then_inc(s_oT, 1)

            def attend(j):
                pe.wait_ge(s_oTs, j + 1)
                pe.matmul(bank[6][:, P:P + D], oT[:], woT[:], start=True, stop=True).then_inc(s_att, 1)

            def turn_xf(j):
                pe.wait_ge(s_xf, j + 1)
                pe.transpose(bank[6][:, 256:384], xf[:, j, :], ident).then_inc(s_xfT, 1)

            def gate(j):
                pe.wait_ge(s_xfTs, j + 1)
                if j >= 1:
                    pe.wait_ge(s_slot, j)
                pe.matmul(bank[7][:, 0:E], xfT[:, P * j:P * j + P], gwT[:], start=True, stop=True).then_inc(s_gate, 1)

            def rank_tokens(j):
                pe.wait_ge(s_sel, j + 1)
                pe.wait_ge(s_top, j + 1)
                last = pe.matmul(bank[7][:, E:2 * E], ltri[:], msel[:], start=True, stop=(j == 0))
                if j >= 1:
                    pe.wait_ge(s_count, j)
                    last = pe.matmul(bank[7][:, E:2 * E], ones[:], msum[:, j - 1, :], start=False, stop=True)
                last.then_inc(s_rank, 1)

            for c in range(NCH + 3):
                a, b, d = c - 1, c - 2, c - 3
                if c == 1:
                    pe.wait_ge(s_tw, 32)
                    pe.transpose(bank[7][:, 0:D], wo, ident)
                    pe.transpose(bank[7][:, D:D + E], gw[0:E, :], ident[0:E, 0:E]).then_inc(s_wTp, 1)
                    pe.wait_ge(s_wT, 2)
                    pe.wait_ge(s_ltri, 1)
                    pe.wait_ge(s_rope, 2)
                    pe.wait_ge(s_qw, 16 * 6)
                    pe.wait_ge(s_pw, 16 * 4)
                project_b, attend_d = 0 <= b < NCH, 0 <= d
                if attend_d:
                    turn_o(d)
                if project_b:
                    turn_xn(b)
                sum_genes(c, 0)
                if attend_d:
                    attend(d)
                if project_b:
                    project(b)
                for n in range(1, 4):
                    sum_genes(c, n)
                if attend_d:
                    turn_xf(d)
                if project_b:
                    turn_qk(b)
                sum_genes(c, 4)
                if attend_d:
                    gate(d)
                if project_b:
                    qkv(b)
                if attend_d:
                    rank_tokens(d)
                for n in range(5, 12):
                    sum_genes(c, n)

            pe.wait_ge(s_sw, 48)
            for i in range(2):
                for a in range(2):
                    last = pe.matmul(bank[2 + 2 * i + a][:], sw13[:, a, :], xfT[:, 512 * i:512 * i + 512], start=True, stop=True)
                last.then_inc(s_sh1, 1)
            pe.wait_ge(s_slot, NCH)
            pe.wait_ge(s_count, NCH)
            pe.matmul(bank[0][:, 0:E], ones[:], msum[:, NCH - 1, :], start=True, stop=True).then_inc(s_total, 1)
            for i in range(2):
                pe.wait_ge(s_shs, i + 1)
                for c in range(4):
                    last = pe.matmul(bank[6 + i][:, c * D:(c + 1) * D], shs[i][:, c * P:(c + 1) * P], sw2s,
                                     start=True, stop=True)
                last.then_inc(s_sh2, 1)

            def turn_xs(g):
                if g % 2 == 0:
                    pe.wait_ge(s_xs[g // 2], 16)
                if g == 0:
                    pe.wait_ge(s_flag, 1)
                if g >= 2:
                    pe.wait_ge(s_xsT, g - 1)
                for i in range(PG):
                    last = pe.transpose(bank[g % 2][:, i * P:(i + 1) * P], xs[:, PG * g + i, :], ident)
                last.then_inc(s_t1, 1)

            def up(g):
                pe.wait_ge(s_xsT, g + 1)
                if g == 0:
                    pe.wait_ge(s_w13, 32)
                    pe.wait_ge(s_shs, 2)
                if g >= 2:
                    pe.wait_ge(s_hm, g - 1)
                for i in range(PG):
                    for par in range(2):
                        last = pe.matmul(bank[2 + g % 2][64 * par:64 * par + 64, i * P:(i + 1) * P],
                                         xsT[g % 2][:, i * P + 64 * par:i * P + 64 * par + 64],
                                         w13[:, 2 * (PG * g + i) + par].rearrange("p a h -> p (a h)"),
                                         start=True, stop=True)
                last.then_inc(s_m1, 1)

            def turn_mid(g):
                pe.wait_ge(s_hm, g + 1)
                if g >= 2:
                    pe.wait_ge(s_hT, g - 1)
                for i in range(PG):
                    last = pe.transpose(bank[4 + g % 2][:, i * P:(i + 1) * P], hm[g % 2][:, i, :], ident)
                last.then_inc(s_t2, 1)

            def down(g):
                pe.wait_ge(s_hT, g + 1)
                if g == 0:
                    pe.wait_ge(s_w2, 32)
                    pe.wait_ge(s_shared, 2)
                if g >= 2:
                    pe.wait_ge(s_ys, g - 1)
                for i in range(PG):
                    last = pe.matmul(bank[6 + g % 2][:, i * D:(i + 1) * D], hT[g % 2][:, i * P:(i + 1) * P],
                                     w2p[:, PG * g + i, :], start=True, stop=True)
                last.then_inc(s_m2, 1)

            turn_xs(0)
            turn_xs(1)
            for g in range(GROUPS):
                up(g)
                if g >= 1:
                    down(g - 1)
                turn_mid(g)
                if g + 2 < GROUPS:
                    turn_xs(g + 2)
            down(GROUPS - 1)

            full = pe.value_load(flag_i[0:1, 0:1], min_val=0, max_val=1)
            with pe.If(full == 1):
                pe.wait_ge(s_fsel, NCH)
                pe.wait_ge(s_ys, GROUPS)
                for j in range(NCH):
                    if j >= 1:
                        pe.wait_ge(s_fgate, j)
                    for i in range(NCH):
                        m = M_UPTO if i < j else M_SAME if i == j else M_BEFORE
                        last = pe.matmul(bank[6][:, 0:E], m_bf[:, m:m + P], sel_bf[:, i, :], start=(i == 0), stop=(i == NCH - 1))
                    last.then_inc(s_fpos, 1)
                with pe.Fori(0, PAIRS) as i:
                    for j in range(NCH):
                        pe.wait_ge(s_facc, i * NCH + (j + 1))
                        pe.matmul(bank[0][:, 0:4 * H], xfT[:, P * j:P * j + P],
                                  w13[:].rearrange("p e a h -> p (e a h)")[:, bass.ds(i * (4 * H), 4 * H)],
                                  start=True, stop=True).then_inc(s_f1, 1)
                        pe.wait_ge(s_fmid, i * NCH + (j + 1))
                        pe.transpose(bank[1][:, 0:P], f_mid, ident).then_inc(s_ft, 1)
                        pe.wait_ge(s_fT, i * NCH + (j + 1))
                        pe.matmul(bank[2][:, 0:D], f_midT, w2p[:].rearrange("p i d -> p (i d)")[:, bass.ds(i * D, D)],
                                  start=True, stop=True).then_inc(s_f2, 1)

        @block.vector
        def _(dve):
            chain = [0]

            def mark(ins):
                chain[0] += 1
                ins.then_inc(s_dve, 1)

            def marked():
                dve.wait_ge(s_dve, chain[0])

            def then(ins):
                mark(ins)
                marked()

            dve.memset(ones[:], 1.0).then_inc(s_ones, 1)
            dve.memset(xrem[0:GREM + 1, :], 1.0).then_inc(s_onesx, 1)

            def turn_rope():
                dve.wait_ge(s_cst, 16)
                dve.wait_ge(s_pw, 64)
                for n, w, wr in ((P, wkr, 0), (QP, wqr, 1)):
                    win = rope_in[0:n, wr, :].rearrange("p (a h r) -> p a r h", a=1, r=R)
                    x1, x2 = (win[:, :, r, :].to_broadcast([n, S, NH]) for r in range(R))
                    cos, sin = (cst[0:n, c:c + S].rearrange("p (s a) -> p s a", a=1).to_broadcast([n, S, NH])
                                for c in (C_COS, C_SIN))
                    tmp = sc[0:n, 0, 0:S * NH].rearrange("p (s h) -> p s h", h=NH)
                    tmp2 = sc[0:n, 1, 0:S * NH].rearrange("p (s h) -> p s h", h=NH)
                    if wr:
                        dve.wait_ge(s_rope, 1)
                    mark(dve.tensor_tensor(w[0:n, :, 0, :], x1, cos, ALU.mult))
                    mark(dve.tensor_tensor(tmp, x2, sin, ALU.mult))
                    mark(dve.tensor_tensor(w[0:n, :, 1, :], x2, cos, ALU.mult))
                    mark(dve.tensor_tensor(tmp2, x1, sin, ALU.mult))
                    marked()
                    dve.tensor_tensor(w[0:n, :, 0, :], w[0:n, :, 0, :], tmp, ALU.subtract)
                    dve.tensor_tensor(w[0:n, :, 1, :], w[0:n, :, 1, :], tmp2, ALU.add).then_inc(s_rope, 1)

            pieces = iter([(j, *piece) for j in range(NCH) for piece in vector_pieces(j)])

            def mask_pieces(n):
                for j, q, a, b in islice(pieces, n):
                    dve.wait_ge(s_ring[(j % 2) * UNITS + q], 16 * (j // 2 + 1))
                    if j == 0 and q % 2 == 0:
                        dve.wait_ge(s_mask[q // 2], 16)
                    m = (q // 2) * UC
                    dve.tensor_tensor(unit(j, q, a, b), unit(j, q, a, b), mask[:, (m + a) * D:(m + b) * D],
                                      ALU.mult).then_inc(s_masked, 1)

            def aggregate(a, b, s_var):
                for i in range(a, b):
                    mark(dve.bn_aggr(mv[:, i, :], stats[:, i, :]))
                marked()
                dve.tensor_scalar(mv[:, a:b, 1], mv[:, a:b, 1], EPS, None, ALU.add).then_inc(s_var, 1)

            def norm(out, v, i):
                return dve.tensor_scalar(out, v, mv[:, i, 0:1], rstd[:, i:i + 1], ALU.subtract, ALU.mult)

            def scores(j):
                n, f = 2 * j + 2, NH * DK
                dve.wait_ge(s_kv, 2 * j + 1)
                if j == 0:
                    dve.wait_ge(s_zero, 32)
                pr = prod[:, 0:n * f].rearrange("p (s f) -> p s f", f=f)
                then(dve.tensor_tensor(pr, kcat[:, 0:n].rearrange("p s h d -> p s (h d)"),
                                       qcat[:].rearrange("p (a h) d -> p a (h d)", a=1).to_broadcast([P, n, f]), ALU.mult))
                then(dve.tensor_reduce(sc[:, 0, 0:n * NH], prod[:, 0:n * f].rearrange("p (s d) -> p s d", d=DK), AX.X, ALU.add))
                then(dve.memset(sc[0:64, 0, (n - 1) * NH:n * NH], NEG))

            def less_max(j):
                n = 2 * j + 2
                sv = sc[:, 0, 0:n * NH].rearrange("p (s h) -> p s h", h=NH)
                then(dve.tensor_reduce(mx[:, 0, :], sv.rearrange("p s h -> p h s"), AX.X, ALU.max))
                dve.tensor_tensor(sc[:, 1, 0:n * NH].rearrange("p (s h) -> p s h", h=NH), sv,
                                  mx[:, 0:1, :].to_broadcast([P, n, NH]), ALU.subtract).then_inc(s_sc, 1)

            def heads(j):
                n = 2 * j + 2
                dve.wait_ge(s_p, j + 1)
                dve.wait_ge(s_kv, 2 * j + 2)
                pv = sc[:, 0, 0:n * NH].rearrange("p (s h) -> p s h", h=NH)
                mark(dve.tensor_reduce(mx[:, 1, :], pv.rearrange("p s h -> p h s"), AX.X, ALU.add))
                pr = prod[:, 0:n * D].rearrange("p (f d) -> p f d", d=DH)
                then(dve.tensor_tensor(pr, vcat[:, 0:n, :].rearrange("p s (h d) -> p (s h) d", d=DH),
                                       sc[:, 0, 0:n * NH].rearrange("p (f a) -> p f a", a=1).to_broadcast([P, n * NH, DH]), ALU.mult))
                mark(dve.reciprocal(mx[:, 2, :], mx[:, 1, :]))
                then(dve.tensor_reduce(o[:, 0, :], prod[:, 0:n * D].rearrange("p (s f) -> p f s", f=D), AX.X, ALU.add))
                dve.tensor_tensor(o[:, 1, :].rearrange("p (h d) -> p h d", d=DH), o[:, 0, :].rearrange("p (h d) -> p h d", d=DH),
                                  mx[:, 2, :].rearrange("p (h a) -> p h a", a=1).to_broadcast([P, NH, DH]), ALU.mult).then_inc(s_o, 1)

            def choose(j):
                dve.wait_ge(s_gate, j + 1)
                then(dve.max(top[:, j, :], bank[7][:, 0:E]))
                if j >= 1:
                    dve.wait_ge(s_rank, j)
                dve.tensor_scalar(msel[:], bank[7][:, 0:E], top[:, j, 1:2], None, ALU.is_ge).then_inc(s_sel, 1)
                dve.max_index(topi[:, j, :], top[:, j, :], bank[7][:, 0:E]).then_inc(s_top, 1)
                dve.wait_ge(s_sel, j + 1)
                if j >= 1:
                    dve.wait_ge(s_count, j)
                    dve.tensor_tensor(msum[:, j, :], msum[:, j - 1, :], msel[:], ALU.add).then_inc(s_count, 1)
                else:
                    dve.tensor_copy(msum[:, 0, :], msel[:]).then_inc(s_count, 1)

            def place(j):
                dve.wait_ge(s_rank, j + 1)
                dve.wait_ge(s_top, j + 1)
                for k in range(2):
                    mark(dve.scalar_tensor_tensor(rjunk[:, k], iota, topi[:, j, k:k + 1], bank[7][:, E:2 * E],
                                                  ALU.is_equal, ALU.mult, accum_out=rank[:, k:k + 1]))
                marked()
                mark(dve.scalar_tensor_tensor(slot[:, j, :], topi[:, j, 0:2], float(SLOTS), rank[:], ALU.mult, ALU.add))
                mark(dve.tensor_scalar(far[:], rank[:], float(SLOTS), FAR, ALU.is_ge, ALU.mult))
                marked()
                dve.tensor_tensor(s_idx[:, j, :], slot[:, j, :], far[:], ALU.add).then_inc(s_slot, 1)

            for c in range(NCH + 3):
                a, b, d = c - 1, c - 2, c - 3
                if c == 0:
                    mask_pieces(LEAD)
                of_a, of_b, of_d = 0 <= a < NCH, 0 <= b < NCH, 0 <= d
                mask_pieces(2)
                if of_d:
                    dve.wait_ge(s_att, d + 1)
                    then(dve.tensor_tensor(hres[:, d, :], hres[:, d, :], bank[6][:, P:P + D], ALU.add))
                    then(dve.bn_stats(stats[:, 3, :], hres[:, d, :]))
                    aggregate(3, 4, s_var_h2)
                if of_b:
                    dve.wait_ge(s_proj, b + 1)
                    mark(dve.bn_stats(stats[:, 1, :], bank[3][:, 0:QP]))
                    mark(dve.bn_stats(stats[:, 2, :], bank[3][:, QP:QP + KVP]))
                    marked()
                    aggregate(1, 3, s_var_qk)
                if c == 0:
                    turn_rope()
                mask_pieces(1)
                if of_d:
                    dve.wait_ge(s_rstd_h2, d + 1)
                    norm(xf[:, d, :], hres[:, d, :], 3).then_inc(s_xf, 1)
                if of_b:
                    dve.wait_ge(s_rstd_qk, b + 1)
                    norm(qkn[:, 0:QP], bank[3][:, 0:QP], 1)
                    norm(qkn[:, QP:], bank[3][:, QP:QP + KVP], 2).then_inc(s_qkn, 1)
                mask_pieces(2)
                mask_pieces(1)
                if of_d:
                    choose(d)
                mask_pieces(1)
                if of_d:
                    place(d)
                if of_b:
                    scores(b)
                mask_pieces(1)
                if of_b:
                    less_max(b)
                if of_a:
                    dve.wait_ge(s_hres, a + 1)
                    then(dve.bn_stats(stats[:, 0, :], hres[:, a, :]))
                    aggregate(0, 1, s_var_h)
                mask_pieces(len(vector_pieces(c)) - 8 if c < NCH else 0)
                if of_b:
                    heads(b)
                if of_a:
                    dve.wait_ge(s_rstd_h, a + 1)
                    norm(xn, hres[:, a, :], 0).then_inc(s_xn, 1)
                if c == 0:
                    dve.wait_ge(s_rem, 32)
                    dve.wait_ge(s_mrem, 16)
                    dve.tensor_tensor(wrem[0:GREM], wrem[0:GREM],
                                      mrem[0:GREM, :].rearrange("p (a n) -> p a n", a=1).to_broadcast([GREM, S, D]),
                                      ALU.mult).then_inc(s_remm, 1)

            dve.tensor_scalar(g_idx[:], slot[:], float(E * SLOTS - 1), None, ALU.min).then_inc(s_gidx, 1)
            dve.wait_ge(s_tok, 3 * NCH)
            for i in range(2):
                dve.memset(hm[i], 0.0).then_inc(s_hmz, 1)
            dve.wait_ge(s_total, 1)
            then(dve.tensor_reduce(flag[:, 0:1], bank[0][:, 0:E], AX.X, ALU.max))
            dve.tensor_scalar(flag_i[:], flag[:, 0:1], float(SLOTS), None, ALU.is_gt).then_inc(s_flag, 1)
            for i in range(2):
                dve.wait_ge(s_ssil, i + 1)
                dve.tensor_tensor(shs[i], ssil[i], bank[3 + 2 * i][:], ALU.mult).then_inc(s_shs, 1)
            for i in range(2):
                dve.wait_ge(s_sh2, i + 1)
                hv = hres[:, 4 * i:4 * i + 4, :].rearrange("p j d -> p (j d)")
                dve.tensor_tensor(hv, hv, bank[6 + i][:], ALU.add).then_inc(s_shared, 1)
            dve.wait_ge(s_exp, 1)
            then(dve.tensor_scalar(ew[:, 1], ew[:, 0], 1.0, None, ALU.add))
            then(dve.reciprocal(ew[:, 2], ew[:, 1]))
            then(dve.scalar_tensor_tensor(ew[:, 0, :, 0], ew[:, 2, :, 0], 1e-20, ew[:, 2, :, 1], ALU.add, ALU.add))
            then(dve.reciprocal(ew[:, 0, :, 1], ew[:, 0, :, 0]))
            for k in range(2):
                mark(dve.scalar_tensor_tensor(wts[:, :, k], ew[:, 2, :, k], ROUTE_SCALE, ew[:, 0, :, 1], ALU.mult, ALU.mult))
            marked()

            def copy_xsT(g):
                dve.wait_ge(s_t1, g + 1)
                if g >= 2:
                    dve.wait_ge(s_m1, g - 1)
                dve.tensor_copy(xsT[g % 2], bank[g % 2][:]).then_inc(s_xsT, 1)

            def mid(g):
                dve.wait_ge(s_sil, g + 1)
                if g == 0:
                    dve.wait_ge(s_hmz, 2)
                if g >= 2:
                    dve.wait_ge(s_t2, g - 1)
                for par in range(2):
                    r = slice(64 * par, 64 * par + 64)
                    last = dve.tensor_tensor(hm[g % 2][r, :, 64 * par:64 * par + 64], sil[g % 2][r],
                                             bank[2 + g % 2][r].rearrange("p (i f) -> p i f", f=2 * H)[:, :, H:2 * H], ALU.mult)
                last.then_inc(s_hm, 1)

            copy_xsT(0)
            for g in range(GROUPS):
                if g + 1 < GROUPS:
                    copy_xsT(g + 1)
                mid(g)
            for j in range(NCH):
                dve.wait_ge(s_yg[j], 32)
                if j == 0:
                    dve.wait_ge(s_shared, 2)
                then(dve.scalar_tensor_tensor(fin[:, j, :], yg[:, 2 * j, :], wts[:, j, 0:1], hres[:, j, :], ALU.mult, ALU.add))
                dve.scalar_tensor_tensor(fin[:, j, :], yg[:, 2 * j + 1, :], wts[:, j, 1:2], fin[:, j, :],
                                         ALU.mult, ALU.add).then_inc(s_fin, 1)

            full = dve.value_load(flag_i[0:1, 0:1], min_val=0, max_val=1)
            with dve.If(full == 1):
                dve.wait_ge(s_fm, 16)
                mark(dve.tensor_copy(m_bf, m_in))
                for j in range(NCH):
                    then(dve.tensor_scalar(pick, iota, topi[:, j, 0:1], None, ALU.is_equal))
                    dve.scalar_tensor_tensor(sel_bf[:, j, :], iota, topi[:, j, 1:2], pick, ALU.is_equal, ALU.add).then_inc(s_fsel, 1)
                    dve.wait_ge(s_fsel, j + 1)
                for j in range(NCH):
                    if j >= 1:
                        dve.wait_ge(s_fgate, j)
                    then(dve.scalar_tensor_tensor(pick, iota, topi[:, j, 0:1], wts[:, j, 0:1].to_broadcast([P, E]),
                                                  ALU.is_equal, ALU.mult))
                    mark(dve.scalar_tensor_tensor(gates[:, j, :], iota, topi[:, j, 1:2], wts[:, j, 1:2].to_broadcast([P, E]),
                                                  ALU.is_equal, ALU.mult))
                    marked()
                    then(dve.tensor_tensor(pick, pick, gates[:, j, :], ALU.add))
                    dve.wait_ge(s_fpos, j + 1)
                    dve.scalar_tensor_tensor(gates[:, j, :], bank[6][:, 0:E], float(CAP), pick, ALU.is_lt, ALU.mult).then_inc(s_fgate, 1)
                dve.wait_ge(s_out, 16 * NCH)
                dve.wait_ge(s_fgate, NCH)
                dve.tensor_copy(fin[:], hres[:]).then_inc(s_facc, 1)
                with dve.Fori(0, PAIRS) as i:
                    for j in range(NCH):
                        dve.wait_ge(s_fsil, i * NCH + (j + 1))
                        dve.tensor_tensor(f_mid.rearrange("p (a h) -> p a h", h=H), f_sil,
                                          bank[0][:, 0:4 * H].rearrange("p (a f) -> p a f", a=2)[:, :, H:2 * H],
                                          ALU.mult).then_inc(s_fg, 1)
                        dve.wait_ge(s_fg, i * NCH + (j + 1))
                        gj = gates[:, j, bass.ds(i * 2, 2)].rearrange("p (a b) -> p a b", b=1)
                        dve.tensor_tensor(f_mid.rearrange("p (a h) -> p a h", h=H), f_mid.rearrange("p (a h) -> p a h", h=H),
                                          gj.to_broadcast([P, 2, H]), ALU.mult).then_inc(s_fmid, 1)
                        dve.wait_ge(s_f2, i * NCH + (j + 1))
                        dve.tensor_tensor(fin[:, j, :], fin[:, j, :], bank[2][:, 0:D], ALU.add).then_inc(s_facc, 1)


_INS = ['x', 'L0_tok_weight', 'L0_tok_bias', 'L0_tok_mask', 'L0_attn_W_dq', 'L0_attn_W_uq', 'L0_attn_W_qr', 'L0_attn_W_dkv',
        'L0_attn_W_ukv', 'L0_attn_W_kr', 'L0_attn_W_o', 'L0_attn_q_ln_g', 'L0_attn_q_ln_b', 'L0_attn_kv_ln_g',
        'L0_attn_kv_ln_b', 'L0_ffn_gate_w', 'L0_ffn_w1', 'L0_ffn_w3', 'L0_ffn_w2', 'L0_ffn_sw1', 'L0_ffn_sw3', 'L0_ffn_sw2']
_OUTS = [((B, S, D), 'float32')]


def kernel(**inputs):
    import numpy as _np
    import concourse.bacc as _bacc
    from concourse import mybir as _mybir
    from concourse.bass_utils import run_bass_kernel_spmd as _run

    nc = _bacc.Bacc("TRN2", target_bir_lowering=False, num_devices=1)
    arrays, args = {}, []
    for name in _INS:
        a = _np.ascontiguousarray(inputs[name])
        arrays[f"in_{name}_dram"] = a
        args.append(nc.dram_tensor(f"in_{name}_dram", a.shape, _mybir.dt.from_np(a.dtype), kind="ExternalInput").ap())
    for name, c in (("consts_dram", shape_constants()), ("masks_dram", order_masks())):
        arrays[name] = c
        args.append(nc.dram_tensor(name, c.shape, _mybir.dt.from_np(c.dtype), kind="ExternalInput").ap())
    for i, (shape, dtype) in enumerate(_OUTS):
        dt = _mybir.dt.from_np(_np.dtype(dtype))
        args.append(nc.dram_tensor(f"out_{i}_dram", shape, dt, kind="ExternalOutput").ap())
    tower_kernel(nc, *args)
    r = _run(nc, [arrays], core_ids=[0])
    got = tuple(r.results[0][f"out_{i}_dram"] for i in range(len(_OUTS)))
    return got[0]
```

```python
import math
from contextlib import ExitStack

from itertools import islice

import numpy as np
import concourse.bass as bass
from concourse import mybir

ALU = mybir.AluOpType
ACT = mybir.ActivationFunctionType
AX = mybir.AxisListType
F32 = mybir.dt.float32
BF16 = mybir.dt.bfloat16
U32 = mybir.dt.uint32
I32 = mybir.dt.int32

P = 128
B, S, G, D = 64, 16, 5000, 128
NCH = 2 * B * (S // 2) // P
GC = G // P
GREM = G - GC * P
UC = GC // 3
UNITS = 6
RING = 2 * UNITS
NH, DH, R = 8, 16, 2
DK = DH + R
QP, KVP, RD = D // 2, 2 * D // 3, D // 8
E, H = 64, 64
SLOTS, SLOTS2 = 64, 32
NCH1 = 6
ROWS = (E * SLOTS, E * SLOTS2)
PAIRS = E // 2
PG = 4
GROUPS1, GROUPS = ROWS[0] // (PG * P), sum(ROWS) // (PG * P)
STEPS_B, STEPS_C = 2, 4
STORED_EARLY = 2
ZERO_FIRST = True
ROUTE_SCALE = 2.5
CAP = 256
LEAD, POOL_LEAD = 3, 0
POOL_UNITS = ((4,), (4,), (2, 4), (2, 4), (2, 4), (2, 4), (2, 4), (2, 4))
POOL_SHARES = (None, (1, 1, 0), (1, 2, 1), (2, 3, 1))
VECTOR_SHARES = (None, (2, 1, 3, 1, 1, 2), (2, 1, 3, 1, 1, 0), (2, 1, 2, 0, 1, 0))
HALVES = ((0, 7), (7, 13))
QUARTERS = ((0, 4), (4, 7), (7, 10), (10, 13))
EPS = 1e-5
NEG = -3.0e38
SCALE = 1.0 / math.sqrt(DK)
FAR = 100000.0

C_ID, C_IOTA, C_COS, C_SIN, C_PAR, C_W = 0, 128, 192, 208, 224, 226
M_BEFORE, M_UPTO, M_SAME, M_W = 0, P, 2 * P, 3 * P


def EXPERTS(g):
    slots = SLOTS if g < GROUPS1 else SLOTS2
    count = PG * P // slots
    return (g if g < GROUPS1 else g - GROUPS1) * count, count, slots


def T_BANK(g):
    return (0, 2)[g % 2]


def U_BANK(g):
    return (1, 5)[g % 2]


def M_BANK(g):
    return (3, 4)[g % 2]


def Y_BANK(g):
    return 7 if g < GROUPS1 else (7, 6)[g % 2]


def shape_constants():
    c = np.zeros((P, C_W), np.float32)
    c[:, C_ID:C_ID + P] = np.eye(P)
    c[:, C_IOTA:C_IOTA + E] = np.arange(E)
    c[:, C_COS:C_COS + S] = np.cos(np.arange(S))
    c[:, C_SIN:C_SIN + S] = np.sin(np.arange(S))
    c[:, C_PAR:C_PAR + 2] = np.arange(P)[:, None] // SLOTS == np.arange(2)[None]
    return c


def order_masks():
    half, batch = np.arange(P) // B, np.arange(P) % B
    m = np.zeros((P, M_W), np.float32)
    m[:, M_BEFORE:M_BEFORE + P] = batch[:, None] < batch[None, :]
    m[:, M_UPTO:M_UPTO + P] = batch[:, None] <= batch[None, :]
    m[:, M_SAME:M_SAME + P] = batch[:, None] * 2 + half[:, None] < batch[None, :] * 2 + half[None, :]
    return m


def tower_kernel(nc, x, tok_w, tok_b, tok_mask, W_dq, W_uq, W_qr, W_dkv, W_ukv, W_kr, W_o,
                 q_ln_g, q_ln_b, kv_ln_g, kv_ln_b, gate_w, w1, w3, w2, sw1, sw3, sw2, consts, masks, out):
    with ExitStack() as ctx:
        def sb(name, shape, dt=F32):
            return ctx.enter_context(nc.sbuf_tensor(name, shape, dt))

        def sem(name):
            return ctx.enter_context(nc.semaphore(name))

        xs_dram, ys_dram = ([nc.dram_tensor(f"expert_{name}_{r + 1}", (ROWS[r], D), F32, kind="Internal").ap()
                             for r in range(2)] for name in ("inputs", "outputs"))

        bank = [ctx.enter_context(nc.psum_tensor(f"bank{i}", [P, 512], F32)) for i in range(8)]
        ring = sb("ring", [P, RING * UC * D])
        mask = sb("mask", [P, GC * D])
        w13 = sb("w13", [P, E, 2, H])
        w2p = sb("w2p", [P, PAIRS, D])
        xT = sb("xT", [P, GC * B])
        xrem = sb("xrem", [P, B])
        cst = sb("cst", [P, C_W])
        ltri = sb("ltri", [P, P], BF16)
        ones = sb("ones", [P, P], BF16)
        wproj = sb("wproj", [P, QP + KVP])
        wuq = sb("wuq", [P, D])
        wukv = sb("wukv", [P, 2 * D])
        lnp = sb("lnp", [P, 4])
        woT = sb("woT", [P, D])
        gwT = sb("gwT", [P, E])
        rope_in = sb("rope_in", [P, 2, RD])
        wkr = sb("wkr", [P, S, R, NH])
        wqr = sb("wqr", [P, S, R, NH])
        half = sb("half", [P, 2])
        hres = sb("hres", [P, NCH, D])
        xf = sb("xf", [P, NCH, D])
        xfT = sb("xfT", [P, NCH * P])
        xnT = sb("xnT", [P, P])
        oT = sb("oT", [P, P])
        stats = sb("stats", [P, 4, 6])
        mv = sb("mv", [P, 4, 2])
        rstd = sb("rstd", [P, 4])
        qkn = sb("qkn", [P, QP + KVP])
        cqT = sb("cqT", [P, P])
        ckvT = sb("ckvT", [P, P])
        kcat = sb("kcat", [P, S, NH, DK])
        vcat = sb("vcat", [P, S, D])
        qcat = sb("qcat", [P, NH, DK])
        prod = sb("prod", [P, S * NH * DK])
        sc = sb("sc", [P, 2, S * NH])
        mx = sb("mx", [P, 3, NH])
        o = sb("o", [P, 2, D])
        top = sb("top", [P, NCH, 8])
        topi = sb("topi", [P, NCH, 8], U32)
        ew = sb("ew", [P, 3, NCH, 2])
        wts = sb("wts", [P, NCH, 2])
        msel = sb("msel", [P, E], BF16)
        flag = sb("flag", [P, 2])
        flag_i = sb("flag_i", [P, 1], I32)
        msum = sb("msum", [P, NCH, E], BF16)
        rank = sb("rank", [P, 2])
        slot = sb("slot", [P, NCH, 2])
        far = sb("far", [P, 2])
        s_idx = sb("scatter_index", [P, NCH, 2], U32)
        g_idx = sb("gather_index", [P, NCH, 2], U32)

        wrem = w2p[0:GREM + 1, 0:S, :]

        def ring_view(a, n):
            return ring[:, a:a + n]
        xs = ring_view(0, sum(ROWS) * D // P).rearrange("p (i d) -> p i d", d=D)
        ys = ring_view(6144, sum(ROWS) * D // P).rearrange("p (i d) -> p i d", d=D)
        yg = ring_view(12288, 2 * NCH * D).rearrange("p (i d) -> p i d", d=D)
        zeros = ring_view(12288, E * SLOTS2 * D // P)
        xsT = [ring_view(14336 + 512 * i, 512) for i in range(2)]
        hT = [ring_view(15360 + 512 * i, 512) for i in range(2)]
        sil = [ring_view(16384 + 256 * i, 256).rearrange("p (i h) -> p i h", h=H) for i in range(2)]
        sw13 = ring_view(16896, 2 * D).rearrange("p (a d) -> p a d", a=2)
        sw2s = ring_view(17152, D)
        fin = ring_view(17280, NCH * D).rearrange("p (j d) -> p j d", d=D)
        ssil, shs = ring_view(18304, 512), ring_view(18816, 512)
        hm = [mask[:, 512 * i:512 * i + 512].rearrange("p (i d) -> p i d", d=D) for i in range(4)]
        gt = [mask[:, 2048 + 512 * i:2560 + 512 * i].rearrange("p (i h) -> p i h", h=2 * H) for i in range(2)]
        xst = w13[0:B].rearrange("p e a h -> p (e a h)")[:, 0:G]

        wo, gw, mrem = hres[:, NCH - 1, :], hres[:, NCH - 2, :], hres[:, NCH - 3, :]
        xn = qkn[:, 0:D]
        rjunk = prod[:, 0:2 * E].rearrange("p (k e) -> p k e", k=2)

        m_in = ring_view(0, M_W)
        m_bf = ring_view(512, M_W // 2).bitcast(BF16)
        sel_bf = ring_view(1024, NCH * E // 2).bitcast(BF16).rearrange("p (j e) -> p j e", e=E)
        pick = ring_view(1536, E)
        gates = ring_view(2048, NCH * E).rearrange("p (j e) -> p j e", e=E)
        f_sil = ring_view(3072, 2 * H).rearrange("p (a h) -> p a h", h=H)
        f_mid = ring_view(3328, 2 * H)
        f_midT = ring_view(3584, P)

        ident = cst[:, C_ID:C_ID + P]
        iota = cst[:, C_IOTA:C_IOTA + E]

        s_x, s_cst, s_rem, s_mrem = sem("x_in"), sem("cst_in"), sem("rem_in"), sem("mrem_in")
        s_pw, s_qw, s_tw, s_sw = sem("proj_w_in"), sem("qkv_w_in"), sem("turned_w_in"), sem("shared_w_in")
        s_mask = [sem(f"mask_in{t}") for t in range(3)]
        s_ring = [sem(f"ring_in{i}") for i in range(RING)]
        s_w13, s_w2 = sem("w13_in"), sem("w2_in")
        s_xs = [sem(f"xs_in{i}") for i in range(GROUPS // 2)]
        s_ones, s_onesx, s_ltri, s_zsrc, s_zero = (sem("ones_set"), sem("ones_row_set"), sem("ltri_set"),
                                                   sem("zero_source"), [sem("slots_zeroed_1"), sem("slots_zeroed_2")])
        s_xTp, s_xTs, s_wTp, s_wT, s_rope = (sem("x_transposed"), sem("xT_copied"), sem("w_transposed"),
                                             sem("wT_copied"), sem("rope_turned"))
        s_masked, s_pmask, s_remm, s_tok = sem("piece_masked"), sem("unit_masked_pool"), sem("rem_masked"), sem("third_summed")
        s_hres = sem("h_kept")
        s_var_h, s_var_qk, s_var_h2 = sem("variance_h"), sem("variance_qk"), sem("variance_h2")
        s_rstd_h, s_rstd_qk, s_rstd_h2 = sem("rstd_h"), sem("rstd_qk"), sem("rstd_h2")
        s_xn, s_xnT, s_xnTs, s_proj = sem("xn"), sem("xn_transposed"), sem("xnT_copied"), sem("projected")
        s_qkn, s_qkT, s_qkTs, s_qkv, s_kv = (sem("qk_normed"), sem("qk_transposed"), sem("qkT_copied"), sem("qkv"),
                                             sem("qkv_copied"))
        s_sc, s_p, s_o, s_oT, s_oTs, s_att = (sem("scores"), sem("probs"), sem("heads"), sem("o_transposed"),
                                              sem("oT_copied"), sem("attended"))
        s_xf, s_xfT, s_xfTs, s_gate = sem("xf"), sem("xf_transposed"), sem("xfT_copied"), sem("gate_logits")
        s_sel, s_count, s_rank, s_slot, s_scat = (sem("selected"), sem("counted_before"), sem("ranked"), sem("slots"),
                                                  [sem("scattered_1"), sem("scattered_2")])
        s_top, s_exp, s_gidx = sem("top2"), sem("top2_exp"), sem("gather_slots")
        s_sh1, s_ssil, s_shs, s_sh2, s_shared = (sem("shared_up"), sem("shared_silu"), sem("shared_mid"),
                                                 sem("shared_down"), sem("shared_added"))
        s_t1, s_xsT, s_m1, s_sil, s_hm, s_t2, s_hT, s_m2, s_ys = (
            sem("xs_transposed"), sem("xsT_copied"), sem("up"), sem("silu"), sem("mid"), sem("mid_transposed"),
            sem("midT_copied"), sem("down"), sem("y_copied"))
        s_hmz = sem("mid_zeroed")
        s_yout = [sem("y_out_1"), sem("y_out_2")]
        s_yg = [sem(f"y_gathered{j}") for j in range(NCH)]
        s_fin, s_out = sem("final"), sem("out")
        s_total, s_flag = sem("expert_totals"), sem("flag")
        s_fm, s_fsel, s_fpos, s_fgate = sem("order_masks_in"), sem("full_selected"), sem("full_positions"), sem("full_gates")
        s_f1, s_fsil, s_fmid, s_ft, s_fT, s_f2, s_facc = (sem("full_up"), sem("full_silu"), sem("full_mid"),
            sem("full_transposed"), sem("full_midT"), sem("full_down"), sem("full_added"))
        s_fg = sem("full_product")
        s_dve, s_pool = sem("vector_chain"), sem("gpsimd_chain")

        tw = tok_w[:, 0:GC * P, :].rearrange("e (p c) n -> e p (c n)", c=GC)
        tm = tok_mask[0:GC * P, :].rearrange("(p c) n -> p (c n)", c=GC)

        def pool_units(j):
            return POOL_UNITS[j]

        def halves(units):
            return [(q, a, b) for t in range(3) for a, b in HALVES for q in (2 * t, 2 * t + 1) if q in units]

        def vector_pieces(j):
            return halves([q for q in range(UNITS) if q not in pool_units(j)])

        def pool_pieces(j):
            return halves(pool_units(j))

        def masked_until(pieces, j, last):
            return sum(len(pieces(i)) for i in range(j)) + pieces(j).index(last) + 1

        def unit(j, q, a=0, b=UC):
            r = (j % 2) * UNITS + q
            return ring[:, (r * UC + a) * D:(r * UC + b) * D]

        block = ctx.enter_context(nc.Block())

        @block.sync
        def _(sp):
            for j in range(NCH):
                for q in range(UNITS):
                    t, par = q // 2, q % 2
                    if j == 0 and par == 0:
                        sp.dma_start(mask[:, t * UC * D:(t + 1) * UC * D],
                                     tm[:, t * UC * D:(t + 1) * UC * D]).then_inc(s_mask[t], 16)
                    if j >= 2:
                        sp.wait_ge(s_tok, 3 * (j - 2) + t + 1)
                    sp.dma_start(unit(j, q), tw[2 * j + par, :, t * UC * D:(t + 1) * UC * D]).then_inc(
                        s_ring[(j % 2) * UNITS + q], 16)
                    if j == 0 and q == 0:
                        sp.dma_start(xst, x).then_inc(s_x, 16)
                    if j == 0 and q == UNITS - 1:
                        sp.dma_start(wrem[0:GREM], tok_w[:, GC * P:G, :].rearrange("e g n -> g e n")).then_inc(s_rem, 16)
                        sp.dma_start(wrem[GREM:GREM + 1], tok_b.rearrange("(a e) n -> a e n", a=1)).then_inc(s_rem, 16)
                        sp.dma_start(mrem[0:GREM, :], tok_mask[GC * P:G, :]).then_inc(s_mrem, 16)
            sp.wait_ge(s_xTp, 5)
            sp.dma_start(w13[:, :, 0, :], w1.rearrange("e d h -> d e h")).then_inc(s_w13, 16)
            sp.dma_start(w13[:, :, 1, :], w3.rearrange("e d h -> d e h")).then_inc(s_w13, 16)
            sp.wait_ge(s_tok, 3 * NCH)
            sp.dma_start(sw13[:, 0, :], sw1).then_inc(s_sw, 16)
            sp.dma_start(sw13[:, 1, :], sw3).then_inc(s_sw, 16)
            sp.dma_start(sw2s, sw2).then_inc(s_sw, 16)
            for par in range(2):
                sp.dma_start(w2p[64 * par:64 * par + 64], w2[par::2].rearrange("i h d -> h i d")).then_inc(s_w2, 16)

            def load_slots(r, i):
                t = 8 * i - (PG * GROUPS1 if r else 0)
                sp.dma_start(xs[:, 8 * i:8 * i + 8, :],
                             xs_dram[r][P * t:P * (t + 8), :].rearrange("(i p) d -> p i d", p=P)).then_inc(s_xs[i], 16)

            def store_group(g):
                r, t = (0, PG * g) if g < GROUPS1 else (1, PG * (g - GROUPS1))
                sp.wait_ge(s_ys, g + 1)
                sp.dma_start(ys_dram[r][P * t:P * (t + PG), :].rearrange("(i p) d -> p i d", p=P),
                             ys[:, PG * g:PG * g + PG, :]).then_inc(s_yout[r], 16)

            def zero_slots():
                sp.wait_ge(s_zsrc, 2)
                sp.dma_start(xs_dram[1].rearrange("(p r) d -> p (r d)", p=P), zeros).then_inc(s_zero[1], 16)

            if ZERO_FIRST:
                zero_slots()
            sp.wait_ge(s_scat[0], 16 * 2 * NCH1)
            for i in range(GROUPS1 // 2):
                load_slots(0, i)
            if not ZERO_FIRST:
                zero_slots()
            for g in range(STORED_EARLY):
                store_group(g)
            sp.wait_ge(s_scat[1], 16 * 2 * (NCH - NCH1))
            for i in range(GROUPS1 // 2, GROUPS // 2):
                load_slots(1, i)
            for g in range(STORED_EARLY, GROUPS):
                store_group(g)

            def write_out():
                for i in range(NCH // 2):
                    sp.wait_ge(s_fin, 2 * i + 2)
                    for par in range(2):
                        sp.dma_start(out[:, 4 * i + par:4 * i + 4:2, :],
                                     fin[64 * par:64 * par + 64, 2 * i:2 * i + 2, :]).then_inc(s_out, 16)

            write_out()
            sp.wait_ge(s_out, 16 * NCH)
            full = sp.value_load(flag_i[0:1, 0:1], min_val=0, max_val=1)
            with sp.If(full == 1):
                sp.wait_ge(s_yout[0], 16 * GROUPS1)
                sp.dma_start(m_in, masks).then_inc(s_fm, 16)
                sp.wait_ge(s_facc, 1 + NCH * PAIRS)
                for par in range(2):
                    sp.dma_start(out[:, par::2, :], fin[64 * par:64 * par + 64]).then_inc(s_out, 16)
                sp.wait_ge(s_out, 16 * (NCH + 2))

        @block.gpsimd
        def _(pool):
            pool.memset(prod[:, 0:2048], 0.0).then_inc(s_zsrc, 1)
            pool.memset(half[:], -0.5).then_inc(s_pool, 1)
            pool.wait_ge(s_ones, 1)
            pool.affine_select(out=ltri[:], in_=ones[:], pattern=[[1, P]], compare_op=ALU.is_ge, fill=0.0,
                               base=-1, channel_multiplier=-1).then_inc(s_ltri, 1)
            pool.wait_ge(s_pool, 1)

            def root(s_var, n, a, b, s_rstd):
                pool.wait_ge(s_var, n)
                pool.tensor_tensor(rstd[:, a:b], mv[:, a:b, 1], half[:, 0:b - a], ALU.pow).then_inc(s_rstd, 1)

            pieces = iter([(j, *piece) for j in range(NCH) for piece in pool_pieces(j)])

            def mask_pieces(n):
                for j, q, a, b in islice(pieces, n):
                    pool.wait_ge(s_ring[(j % 2) * UNITS + q], 16 * (j // 2 + 1))
                    if j == 0:
                        pool.wait_ge(s_mask[q // 2], 16)
                    m = (q // 2) * UC
                    pool.tensor_tensor(unit(j, q, a, b), unit(j, q, a, b), mask[:, (m + a) * D:(m + b) * D],
                                       ALU.mult).then_inc(s_pmask, 1)

            def root_h(j):
                root(s_var_h, j + 1, 0, 1, s_rstd_h)

            def root_qk(j):
                root(s_var_qk, j + 1, 1, 3, s_rstd_qk)

            def root_h2(j):
                root(s_var_h2, j + 1, 3, 4, s_rstd_h2)

            def scatter(j):
                if j == 0:
                    pool.wait_ge(s_zero[0], 32)
                if j == NCH1:
                    pool.wait_ge(s_zero[1], 16)
                pool.wait_ge(s_slot, j + 1)
                for k in range(2):
                    pool.indirect_dma_start(
                        out=xs_dram[j // NCH1], out_offset=bass.IndirectOffsetOnAxis(ap=s_idx[:, j, k:k + 1], axis=0),
                        in_=xf[:, j, :], in_offset=None, bounds_check=ROWS[j // NCH1] - 1, oob_is_err=False).then_inc(s_scat[j // NCH1], 16)

            mask_pieces(POOL_LEAD)
            for c in range(NCH):
                b, d = c - 2, c - 3
                share = POOL_SHARES[len(pool_units(c))]
                mask_pieces(share[0])
                if d >= 0:
                    root_h2(d)
                if b >= 0:
                    root_qk(b)
                mask_pieces(share[1])
                if d >= 0:
                    scatter(d)
                mask_pieces(share[2])
                if c >= 1:
                    root_h(c - 1)

            def mid(g):
                pool.wait_ge(s_sil, g + 1)
                if g >= 2:
                    pool.wait_ge(s_t2, g - 1)
                pool.tensor_tensor(hm[g % 2].rearrange("p i (a h) -> p i a h", a=2),
                                   sil[g % 2].rearrange("p i (a h) -> p i a h", a=1).to_broadcast([P, PG, 2, H]),
                                   gt[g % 2].rearrange("p i (a h) -> p i a h", a=2), ALU.mult).then_inc(s_hm, 1)

            pool.wait_ge(s_tok, 3 * NCH)
            pool.memset(zeros, 0.0).then_inc(s_zsrc, 1)
            root_h2(NCH - 3)
            root_qk(NCH - 2)
            root_h(NCH - 1)
            scatter(NCH - 3)
            for i in range(2):
                pool.memset(hm[2 + i], 0.0).then_inc(s_hmz, 1)
            root_qk(NCH - 1)
            root_h2(NCH - 2)
            scatter(NCH - 2)
            for g in range(STEPS_C):
                mid(g)
            root_h2(NCH - 1)
            scatter(NCH - 1)
            for g in range(STEPS_C, GROUPS1):
                mid(g)
            for r in range(2):
                pool.wait_ge(s_gidx, r + 1)
                pool.wait_ge(s_yout[r], 16 * (GROUPS1 if r == 0 else GROUPS - GROUPS1))
                for j in range(NCH1) if r == 0 else range(NCH1, NCH):
                    for k in range(2):
                        pool.indirect_dma_start(
                            out=yg[:, 2 * j + k, :], out_offset=None, in_=ys_dram[r],
                            in_offset=bass.IndirectOffsetOnAxis(ap=g_idx[:, j, k:k + 1], axis=0),
                            bounds_check=ROWS[r] - 1, oob_is_err=False).then_inc(s_yg[j], 16)

        @block.scalar
        def _(act):
            act.dma_start(cst[:], consts).then_inc(s_cst, 16)
            act.dma_start(wproj[:, 0:QP], W_dq).then_inc(s_pw, 16)
            act.dma_start(wproj[:, QP:QP + KVP], W_dkv).then_inc(s_pw, 16)
            act.dma_start(rope_in[:, 0, :], W_kr).then_inc(s_pw, 16)
            act.dma_start(rope_in[0:QP, 1, :], W_qr).then_inc(s_pw, 16)
            act.dma_start(wuq[0:QP, :], W_uq).then_inc(s_qw, 16)
            act.dma_start(wukv[0:KVP, :], W_ukv).then_inc(s_qw, 16)
            for i, (v, n) in enumerate(((q_ln_g, QP), (q_ln_b, QP), (kv_ln_g, KVP), (kv_ln_b, KVP))):
                act.dma_start(lnp[0:n, i:i + 1], v.rearrange("(n a) -> n a", a=1)).then_inc(s_qw, 16)
            act.dma_start(wo, W_o).then_inc(s_tw, 16)
            act.dma_start(gw[0:E, :], gate_w).then_inc(s_tw, 16)
            act.wait_ge(s_zsrc, 1)
            for i in range(2):
                act.dma_start(xs_dram[0].rearrange("(p r) d -> p (r d)", p=P)[:, 2048 * i:2048 * (i + 1)],
                              prod[:, 0:2048]).then_inc(s_zero[0], 16)
            for i in range(5):
                act.wait_ge(s_xTp, i + 1)
                w = min(8, GC - 8 * i) * B
                act.copy(xT[:, 512 * i:512 * i + w], bank[i][:, 0:w]).then_inc(s_xTs, 1)
            act.wait_ge(s_onesx, 1)
            act.copy(xrem[0:GREM, :], bank[4][0:GREM, 448:512]).then_inc(s_xTs, 1)
            def keep_h(j):
                act.wait_ge(s_tok, 3 * j + 3)
                act.copy(hres[:, j, :], bank[j % 2][:, 0:D]).then_inc(s_hres, 1)

            def copy_xnT(j):
                act.wait_ge(s_xnT, j + 1)
                act.copy(xnT[:], bank[2][:, 0:P]).then_inc(s_xnTs, 1)

            def copy_qkv(j):
                act.wait_ge(s_qkT, j + 1)
                act.activation(cqT[0:QP, :], bank[2][0:QP, 0:P], ACT.Identity, bias=lnp[0:QP, 1:2], scale=lnp[0:QP, 0:1])
                act.activation(ckvT[0:KVP, :], bank[2][0:KVP, P:2 * P], ACT.Identity,
                               bias=lnp[0:KVP, 3:4], scale=lnp[0:KVP, 2:3]).then_inc(s_qkTs, 1)
                act.wait_ge(s_qkv, j + 1)
                act.copy(kcat[:, 2 * j:2 * j + 2, :, DH:DK].rearrange("p a h r -> p a r h"),
                         bank[3][:, D + RD:D + 3 * RD].rearrange("p (a r h) -> p a r h", a=2, r=R))
                act.copy(qcat[:, :, 0:DH], bank[3][:, 0:D].rearrange("p (h d) -> p h d", d=DH))
                act.copy(qcat[:, :, DH:DK].rearrange("p h r -> p r h"), bank[3][:, D:D + RD].rearrange("p (r h) -> p r h", r=R))
                act.copy(kcat[:, 2 * j:2 * j + 2, :, 0:DH],
                         bank[4][:].rearrange("p (a f) -> p a f", a=2)[:, :, 0:D].rearrange("p a (h d) -> p a h d", d=DH)
                         ).then_inc(s_kv, 1)
                act.copy(vcat[:, 2 * j:2 * j + 2, :],
                         bank[4][:].rearrange("p (a f) -> p a f", a=2)[:, :, D:2 * D]).then_inc(s_kv, 1)

            def probs(j):
                n = 2 * j + 2
                act.wait_ge(s_sc, j + 1)
                act.activation(sc[:, 0, 0:n * NH], sc[:, 1, 0:n * NH], ACT.Exp, scale=SCALE).then_inc(s_p, 1)

            def copy_oT(j):
                act.wait_ge(s_oT, j + 1)
                act.copy(oT[:], bank[6][:, 0:P]).then_inc(s_oTs, 1)

            def copy_xfT(j):
                act.wait_ge(s_xfT, j + 1)
                act.copy(xfT[:, P * j:P * j + P], bank[6][:, 256:384]).then_inc(s_xfTs, 1)

            act.wait_ge(s_qw, 16 * 6)
            for c in range(NCH):
                a, b, d = c - 1, c - 2, c - 3
                if c == 1:
                    act.wait_ge(s_wTp, 1)
                    act.copy(woT[:], bank[7][:, 0:D]).then_inc(s_wT, 1)
                    act.copy(gwT[:], bank[7][:, D:D + E]).then_inc(s_wT, 1)
                if d >= 0:
                    copy_oT(d)
                if b >= 0:
                    copy_xnT(b)
                if d >= 0:
                    copy_xfT(d)
                if b >= 0:
                    copy_qkv(b)
                if a >= 0:
                    keep_h(a)
                if b >= 0:
                    probs(b)

            def copy_xsT(g):
                act.wait_ge(s_t1, g + 1)
                if g >= 2:
                    act.wait_ge(s_m1, g - 1)
                act.copy(xsT[g % 2], bank[T_BANK(g)][:]).then_inc(s_xsT, 1)

            def silu(g):
                act.wait_ge(s_m1, g + 1)
                if g >= 2:
                    act.wait_ge(s_hm, g - 1)
                both = bank[U_BANK(g)][:].rearrange("p (i f) -> p i f", f=2 * H)
                if g < GROUPS1:
                    for par in range(2):
                        act.activation(gt[g % 2][:, :, H * par:H * par + H], both[:, :, H:2 * H], ACT.Identity,
                                       scale=cst[:, C_PAR + par:C_PAR + par + 1])
                act.activation(sil[g % 2], both[:, :, 0:H], ACT.Silu).then_inc(s_sil, 1)

            def copy_midT(g):
                act.wait_ge(s_t2, g + 1)
                if g >= 2:
                    act.wait_ge(s_m2, g - 1)
                act.copy(hT[g % 2], bank[M_BANK(g)][:]).then_inc(s_hT, 1)

            def copy_y(g):
                act.wait_ge(s_m2, g + 1)
                act.copy(ys[:, PG * g:PG * g + PG, :], bank[Y_BANK(g)][:].rearrange("p (i d) -> p i d", d=D)).then_inc(s_ys, 1)

            def expert_steps(first, last):
                for g in range(first, last):
                    if g == 0:
                        copy_xsT(0)
                        copy_xsT(1)
                    if g < GROUPS:
                        silu(g)
                    if g + 2 < GROUPS1:
                        copy_xsT(g + 2)
                    if 1 <= g <= GROUPS:
                        copy_midT(g - 1)
                    if g >= 2:
                        copy_y(g - 2)

            def silu_shared(i):
                act.wait_ge(s_sh1, i + 1)
                act.activation(ssil, bank[0][:], ACT.Silu).then_inc(s_ssil, 1)

            keep_h(NCH - 1)
            copy_oT(NCH - 3)
            copy_xnT(NCH - 2)
            copy_xfT(NCH - 3)
            copy_qkv(NCH - 2)
            copy_xnT(NCH - 1)
            probs(NCH - 2)
            silu_shared(0)
            copy_oT(NCH - 2)
            copy_qkv(NCH - 1)
            copy_xfT(NCH - 2)
            expert_steps(0, STEPS_B)
            probs(NCH - 1)
            expert_steps(STEPS_B, STEPS_C)
            copy_oT(NCH - 1)
            copy_xfT(NCH - 1)
            expert_steps(STEPS_C, GROUPS + 2)
            silu_shared(1)
            act.wait_ge(s_top, NCH)
            act.activation(ew[:, 0], top[:, :, 0:2], ACT.Exp, scale=-1.0).then_inc(s_exp, 1)

            act.wait_ge(s_flag, 1)
            full = act.value_load(flag_i[0:1, 0:1], min_val=0, max_val=1)
            with act.If(full == 1):
                with act.Fori(0, PAIRS) as i:
                    for j in range(NCH):
                        act.wait_ge(s_f1, i * NCH + (j + 1))
                        act.activation(f_sil, bank[0][:, 0:4 * H].rearrange("p (a f) -> p a f", a=2)[:, :, 0:H],
                                       ACT.Silu).then_inc(s_fsil, 1)
                        act.wait_ge(s_ft, i * NCH + (j + 1))
                        act.copy(f_midT, bank[1][:, 0:P]).then_inc(s_fT, 1)

        @block.tensor
        def _(pe):
            pe.wait_ge(s_cst, 16)
            pe.wait_ge(s_x, 16)
            for c in range(GC):
                last = pe.transpose(bank[c // 8][:, (c % 8) * B:(c % 8 + 1) * B], xst[:, c:GC * P:GC], ident[0:B, 0:B])
                if c % 8 == 7:
                    last.then_inc(s_xTp, 1)
            pe.transpose(bank[4][0:GREM, 448:512], xst[:, GC * P:G], ident[0:B, 0:B]).then_inc(s_xTp, 1)
            pe.wait_ge(s_xTs, 6)

            def sum_genes(j, n):
                if j >= NCH:
                    return
                t, (a, b) = n // 4, QUARTERS[n % 4]
                half = next(h for h in HALVES if b <= h[1])
                for q in (2 * t, 2 * t + 1):
                    s_done, pieces = (s_pmask, pool_pieces) if q in pool_units(j) else (s_masked, vector_pieces)
                    pe.wait_ge(s_done, masked_until(pieces, j, (q, *half)))
                if t == 0 and a == 0 and j >= 2:
                    pe.wait_ge(s_hres, j - 1)
                for c in range(a, b):
                    for par in range(2):
                        last = pe.matmul(bank[j % 2][64 * par:64 * par + 64, 0:D], xT[:, (UC * t + c) * B:(UC * t + c + 1) * B],
                                         unit(j, 2 * t + par, c, c + 1), start=(t == 0 and c == 0), stop=False)
                if n == 11:
                    if j == 0:
                        pe.wait_ge(s_remm, 1)
                        pe.wait_ge(s_rem, 32)
                    for par in range(2):
                        last = pe.matmul(bank[j % 2][64 * par:64 * par + 64, 0:D], xrem[0:GREM + 1, :],
                                         wrem[:, 2 * j + par, :], start=False, stop=True)
                if n % 4 == 3:
                    last.then_inc(s_tok, 1)

            def turn_xn(j):
                pe.wait_ge(s_xn, j + 1)
                pe.transpose(bank[2][:, 0:P], xn, ident).then_inc(s_xnT, 1)

            def project(j):
                pe.wait_ge(s_xnTs, j + 1)
                if j >= 1:
                    pe.wait_ge(s_kv, 2 * j)
                pe.matmul(bank[3][:, 0:QP + KVP], xnT[:], wproj[:], start=True, stop=True).then_inc(s_proj, 1)

            def turn_qk(j):
                pe.wait_ge(s_qkn, j + 1)
                pe.transpose(bank[2][0:QP, 0:P], qkn[:, 0:QP], ident)
                pe.transpose(bank[2][0:KVP, P:2 * P], qkn[:, QP:], ident).then_inc(s_qkT, 1)

            def qkv(j):
                pe.wait_ge(s_qkTs, j + 1)
                for hf in range(2):
                    pe.matmul(bank[3][64 * hf:64 * hf + 64, D:D + RD], cqT[0:QP, 64 * hf:64 * hf + 64],
                              wqr[0:QP, 2 * j + hf].rearrange("p r h -> p (r h)"), start=True, stop=True)
                pe.matmul(bank[3][:, 0:D], cqT[0:QP, :], wuq[0:QP, :], start=True, stop=True)
                for par in range(2):
                    for hf in range(2):
                        pe.matmul(bank[3][64 * hf:64 * hf + 64, D + RD + RD * par:D + 2 * RD + RD * par],
                                  xnT[:, 64 * par:64 * par + 64], wkr[:, 2 * j + par].rearrange("p r h -> p (r h)"),
                                  start=True, stop=True)
                for par in range(2):
                    for hf in range(2):
                        last = pe.matmul(bank[4][64 * hf:64 * hf + 64, 256 * par:256 * par + 256],
                                         ckvT[0:KVP, 64 * par:64 * par + 64], wukv[0:KVP, :], start=True, stop=True)
                last.then_inc(s_qkv, 1)

            def turn_o(j):
                pe.wait_ge(s_o, j + 1)
                if j >= 1:
                    pe.wait_ge(s_slot, j)
                pe.transpose(bank[6][:, 0:P], o[:, 1, :], ident).then_inc(s_oT, 1)

            def attend(j):
                pe.wait_ge(s_oTs, j + 1)
                pe.matmul(bank[6][:, P:P + D], oT[:], woT[:], start=True, stop=True).then_inc(s_att, 1)

            def turn_xf(j):
                pe.wait_ge(s_xf, j + 1)
                pe.transpose(bank[6][:, 256:384], xf[:, j, :], ident).then_inc(s_xfT, 1)

            def gate(j):
                pe.wait_ge(s_xfTs, j + 1)
                pe.matmul(bank[6][:, 384:384 + E], xfT[:, P * j:P * j + P], gwT[:], start=True, stop=True).then_inc(s_gate, 1)

            def rank_tokens(j):
                pe.wait_ge(s_sel, j + 1)
                pe.wait_ge(s_top, j + 1)
                last = pe.matmul(bank[6][:, 448:448 + E], ltri[:], msel[:], start=True, stop=(j in (0, NCH1)))
                if j not in (0, NCH1):
                    pe.wait_ge(s_count, j)
                    last = pe.matmul(bank[6][:, 448:448 + E], ones[:], msum[:, j - 1, :], start=False, stop=True)
                last.then_inc(s_rank, 1)

            for c in range(NCH):
                b, d = c - 2, c - 3
                if c == 1:
                    pe.wait_ge(s_tw, 32)
                    pe.transpose(bank[7][:, 0:D], wo, ident)
                    pe.transpose(bank[7][:, D:D + E], gw[0:E, :], ident[0:E, 0:E]).then_inc(s_wTp, 1)
                    pe.wait_ge(s_wT, 2)
                    pe.wait_ge(s_ltri, 1)
                    pe.wait_ge(s_rope, 2)
                    pe.wait_ge(s_qw, 16 * 6)
                    pe.wait_ge(s_pw, 16 * 4)
                project_b, attend_d = b >= 0, d >= 0
                if attend_d:
                    turn_o(d)
                if project_b:
                    turn_xn(b)
                sum_genes(c, 0)
                if attend_d:
                    attend(d)
                if project_b:
                    project(b)
                for n in range(1, 4):
                    sum_genes(c, n)
                if attend_d:
                    turn_xf(d)
                if project_b:
                    turn_qk(b)
                sum_genes(c, 4)
                if attend_d:
                    gate(d)
                if project_b:
                    qkv(b)
                if attend_d:
                    rank_tokens(d)
                for n in range(5, 12):
                    sum_genes(c, n)

            def turn_xs(g):
                if g % 2 == 0:
                    pe.wait_ge(s_xs[g // 2], 16)
                if g >= 2:
                    pe.wait_ge(s_xsT, g - 1)
                for i in range(PG):
                    last = pe.transpose(bank[T_BANK(g)][:, i * P:(i + 1) * P], xs[:, PG * g + i, :], ident)
                last.then_inc(s_t1, 1)

            def up(g):
                first, count, slots = EXPERTS(g)
                pe.wait_ge(s_xsT, g + 1)
                if g == 0:
                    pe.wait_ge(s_w13, 32)
                    pe.wait_ge(s_shared, 1)
                if g >= 2:
                    pe.wait_ge(s_hm, g - 1)
                for l in range(count):
                    row, tile = l * slots % P, l * slots // P
                    last = pe.matmul(bank[U_BANK(g)][row:row + slots, tile * P:(tile + 1) * P],
                                     xsT[g % 2][:, l * slots:(l + 1) * slots],
                                     w13[:, first + l].rearrange("p a h -> p (a h)"), start=True, stop=True)
                last.then_inc(s_m1, 1)

            def turn_mid(g):
                pe.wait_ge(s_hm, g + 1)
                if g >= 2:
                    pe.wait_ge(s_hT, g - 1)
                for i in range(PG):
                    last = pe.transpose(bank[M_BANK(g)][:, i * P:(i + 1) * P], hm[g // GROUPS1 * 2 + g % 2][:, i, :], ident)
                last.then_inc(s_t2, 1)

            def down(g):
                first, count, slots = EXPERTS(g)
                pe.wait_ge(s_hT, g + 1)
                if g == 0:
                    pe.wait_ge(s_w2, 32)
                if g >= 1:
                    pe.wait_ge(s_ys, g if g <= GROUPS1 else g - 1)
                if g == GROUPS1 + 1:
                    pe.wait_ge(s_flag, 1)
                for n in range(count // 2):
                    row, tile = 2 * n * slots % P, 2 * n * slots // P
                    last = pe.matmul(bank[Y_BANK(g)][row:row + 2 * slots, tile * D:(tile + 1) * D],
                                     hT[g % 2][:, 2 * n * slots:2 * (n + 1) * slots], w2p[:, first // 2 + n, :],
                                     start=True, stop=True)
                last.then_inc(s_m2, 1)

            def expert_steps(first, last):
                for g in range(first, last):
                    if g == 0:
                        turn_xs(0)
                        turn_xs(1)
                    if g < GROUPS:
                        up(g)
                    if 1 <= g <= GROUPS:
                        turn_mid(g - 1)
                    if g >= 2:
                        down(g - 2)
                    if g + 2 < GROUPS:
                        turn_xs(g + 2)

            def shared(i):
                if i == 0:
                    pe.wait_ge(s_sw, 48)
                    pe.wait_ge(s_hres, NCH)
                else:
                    pe.wait_ge(s_xsT, GROUPS)
                    pe.wait_ge(s_hm, GROUPS)
                for a in range(2):
                    last = pe.matmul(bank[a][:], sw13[:, a, :], xfT[:, 512 * i:512 * i + 512], start=True, stop=True)
                last.then_inc(s_sh1, 1)
                pe.wait_ge(s_shs, i + 1)
                for c in range(4):
                    last = pe.matmul(bank[5][:, c * D:(c + 1) * D], shs[:, c * P:(c + 1) * P], sw2s, start=True, stop=True)
                last.then_inc(s_sh2, 1)

            j, k, l = NCH - 3, NCH - 2, NCH - 1
            turn_o(j)
            turn_xn(k)
            attend(j)
            project(k)
            turn_xf(j)
            turn_qk(k)
            gate(j)
            qkv(k)
            rank_tokens(j)
            turn_xn(l)
            project(l)
            shared(0)
            turn_o(k)
            turn_qk(l)
            attend(k)
            qkv(l)
            turn_xf(k)
            gate(k)
            rank_tokens(k)
            expert_steps(0, STEPS_C)
            turn_o(l)
            attend(l)
            turn_xf(l)
            gate(l)
            rank_tokens(l)
            expert_steps(STEPS_C, GROUPS1)
            pe.wait_ge(s_slot, NCH)
            pe.wait_ge(s_count, NCH)
            pe.matmul(bank[6][:, 0:E], ones[:], msum[:, NCH1 - 1, :], start=True, stop=True)
            pe.matmul(bank[6][:, E:2 * E], ones[:], msum[:, NCH - 1, :], start=True, stop=True).then_inc(s_total, 1)
            expert_steps(GROUPS1, GROUPS + 2)
            shared(1)

            full = pe.value_load(flag_i[0:1, 0:1], min_val=0, max_val=1)
            with pe.If(full == 1):
                pe.wait_ge(s_fsel, NCH)
                pe.wait_ge(s_ys, GROUPS)
                for j in range(NCH):
                    if j >= 1:
                        pe.wait_ge(s_fgate, j)
                    for i in range(NCH):
                        m = M_UPTO if i < j else M_SAME if i == j else M_BEFORE
                        last = pe.matmul(bank[6][:, 0:E], m_bf[:, m:m + P], sel_bf[:, i, :], start=(i == 0), stop=(i == NCH - 1))
                    last.then_inc(s_fpos, 1)
                with pe.Fori(0, PAIRS) as i:
                    for j in range(NCH):
                        pe.wait_ge(s_facc, i * NCH + (j + 1))
                        pe.matmul(bank[0][:, 0:4 * H], xfT[:, P * j:P * j + P],
                                  w13[:].rearrange("p e a h -> p (e a h)")[:, bass.ds(i * (4 * H), 4 * H)],
                                  start=True, stop=True).then_inc(s_f1, 1)
                        pe.wait_ge(s_fmid, i * NCH + (j + 1))
                        pe.transpose(bank[1][:, 0:P], f_mid, ident).then_inc(s_ft, 1)
                        pe.wait_ge(s_fT, i * NCH + (j + 1))
                        pe.matmul(bank[2][:, 0:D], f_midT, w2p[:].rearrange("p i d -> p (i d)")[:, bass.ds(i * D, D)],
                                  start=True, stop=True).then_inc(s_f2, 1)

        @block.vector
        def _(dve):
            chain = [0]

            def mark(ins):
                chain[0] += 1
                ins.then_inc(s_dve, 1)

            def marked():
                dve.wait_ge(s_dve, chain[0])

            def then(ins):
                mark(ins)
                marked()

            dve.memset(ones[:], 1.0).then_inc(s_ones, 1)
            dve.memset(xrem[0:GREM + 1, :], 1.0).then_inc(s_onesx, 1)

            def turn_rope():
                dve.wait_ge(s_cst, 16)
                dve.wait_ge(s_pw, 64)
                for n, w, wr in ((P, wkr, 0), (QP, wqr, 1)):
                    win = rope_in[0:n, wr, :].rearrange("p (a h r) -> p a r h", a=1, r=R)
                    x1, x2 = (win[:, :, r, :].to_broadcast([n, S, NH]) for r in range(R))
                    cos, sin = (cst[0:n, c:c + S].rearrange("p (s a) -> p s a", a=1).to_broadcast([n, S, NH])
                                for c in (C_COS, C_SIN))
                    tmp = sc[0:n, 0, 0:S * NH].rearrange("p (s h) -> p s h", h=NH)
                    tmp2 = sc[0:n, 1, 0:S * NH].rearrange("p (s h) -> p s h", h=NH)
                    if wr:
                        dve.wait_ge(s_rope, 1)
                    mark(dve.tensor_tensor(w[0:n, :, 0, :], x1, cos, ALU.mult))
                    mark(dve.tensor_tensor(tmp, x2, sin, ALU.mult))
                    mark(dve.tensor_tensor(w[0:n, :, 1, :], x2, cos, ALU.mult))
                    mark(dve.tensor_tensor(tmp2, x1, sin, ALU.mult))
                    marked()
                    dve.tensor_tensor(w[0:n, :, 0, :], w[0:n, :, 0, :], tmp, ALU.subtract)
                    dve.tensor_tensor(w[0:n, :, 1, :], w[0:n, :, 1, :], tmp2, ALU.add).then_inc(s_rope, 1)

            pieces = iter([(j, *piece) for j in range(NCH) for piece in vector_pieces(j)])

            def mask_pieces(n):
                for j, q, a, b in islice(pieces, n):
                    dve.wait_ge(s_ring[(j % 2) * UNITS + q], 16 * (j // 2 + 1))
                    if j == 0 and q % 2 == 0:
                        dve.wait_ge(s_mask[q // 2], 16)
                    m = (q // 2) * UC
                    dve.tensor_tensor(unit(j, q, a, b), unit(j, q, a, b), mask[:, (m + a) * D:(m + b) * D],
                                      ALU.mult).then_inc(s_masked, 1)

            def aggregate(a, b, s_var):
                for i in range(a, b):
                    mark(dve.bn_aggr(mv[:, i, :], stats[:, i, :]))
                marked()
                dve.tensor_scalar(mv[:, a:b, 1], mv[:, a:b, 1], EPS, None, ALU.add).then_inc(s_var, 1)

            def norm(out, v, i):
                return dve.tensor_scalar(out, v, mv[:, i, 0:1], rstd[:, i:i + 1], ALU.subtract, ALU.mult)

            def scores(j):
                n, f = 2 * j + 2, NH * DK
                dve.wait_ge(s_kv, 2 * j + 1)
                if j == 0:
                    dve.wait_ge(s_zero[0], 32)
                pr = prod[:, 0:n * f].rearrange("p (s f) -> p s f", f=f)
                then(dve.tensor_tensor(pr, kcat[:, 0:n].rearrange("p s h d -> p s (h d)"),
                                       qcat[:].rearrange("p (a h) d -> p a (h d)", a=1).to_broadcast([P, n, f]), ALU.mult))
                then(dve.tensor_reduce(sc[:, 0, 0:n * NH], prod[:, 0:n * f].rearrange("p (s d) -> p s d", d=DK), AX.X, ALU.add))
                then(dve.memset(sc[0:64, 0, (n - 1) * NH:n * NH], NEG))

            def less_max(j):
                n = 2 * j + 2
                sv = sc[:, 0, 0:n * NH].rearrange("p (s h) -> p s h", h=NH)
                then(dve.tensor_reduce(mx[:, 0, :], sv.rearrange("p s h -> p h s"), AX.X, ALU.max))
                dve.tensor_tensor(sc[:, 1, 0:n * NH].rearrange("p (s h) -> p s h", h=NH), sv,
                                  mx[:, 0:1, :].to_broadcast([P, n, NH]), ALU.subtract).then_inc(s_sc, 1)

            def heads(j):
                n = 2 * j + 2
                dve.wait_ge(s_p, j + 1)
                dve.wait_ge(s_kv, 2 * j + 2)
                pv = sc[:, 0, 0:n * NH].rearrange("p (s h) -> p s h", h=NH)
                mark(dve.tensor_reduce(mx[:, 1, :], pv.rearrange("p s h -> p h s"), AX.X, ALU.add))
                pr = prod[:, 0:n * D].rearrange("p (f d) -> p f d", d=DH)
                then(dve.tensor_tensor(pr, vcat[:, 0:n, :].rearrange("p s (h d) -> p (s h) d", d=DH),
                                       sc[:, 0, 0:n * NH].rearrange("p (f a) -> p f a", a=1).to_broadcast([P, n * NH, DH]), ALU.mult))
                mark(dve.reciprocal(mx[:, 2, :], mx[:, 1, :]))
                then(dve.tensor_reduce(o[:, 0, :], prod[:, 0:n * D].rearrange("p (s f) -> p f s", f=D), AX.X, ALU.add))
                dve.tensor_tensor(o[:, 1, :].rearrange("p (h d) -> p h d", d=DH), o[:, 0, :].rearrange("p (h d) -> p h d", d=DH),
                                  mx[:, 2, :].rearrange("p (h a) -> p h a", a=1).to_broadcast([P, NH, DH]), ALU.mult).then_inc(s_o, 1)

            def stats_h(j):
                dve.wait_ge(s_hres, j + 1)
                then(dve.bn_stats(stats[:, 0, :], hres[:, j, :]))
                aggregate(0, 1, s_var_h)

            def norm_h(j):
                dve.wait_ge(s_rstd_h, j + 1)
                if j >= 1:
                    dve.wait_ge(s_qkT, j)
                norm(xn, hres[:, j, :], 0).then_inc(s_xn, 1)

            def stats_qk(j):
                dve.wait_ge(s_proj, j + 1)
                mark(dve.bn_stats(stats[:, 1, :], bank[3][:, 0:QP]))
                mark(dve.bn_stats(stats[:, 2, :], bank[3][:, QP:QP + KVP]))
                marked()
                aggregate(1, 3, s_var_qk)

            def norm_qk(j):
                dve.wait_ge(s_rstd_qk, j + 1)
                norm(qkn[:, 0:QP], bank[3][:, 0:QP], 1)
                norm(qkn[:, QP:], bank[3][:, QP:QP + KVP], 2).then_inc(s_qkn, 1)

            def add_attended(j):
                dve.wait_ge(s_att, j + 1)
                then(dve.tensor_tensor(hres[:, j, :], hres[:, j, :], bank[6][:, P:P + D], ALU.add))
                then(dve.bn_stats(stats[:, 3, :], hres[:, j, :]))
                aggregate(3, 4, s_var_h2)

            def norm_xf(j):
                dve.wait_ge(s_rstd_h2, j + 1)
                norm(xf[:, j, :], hres[:, j, :], 3).then_inc(s_xf, 1)

            def choose(j):
                dve.wait_ge(s_gate, j + 1)
                then(dve.max(top[:, j, :], bank[6][:, 384:384 + E]))
                if j >= 1:
                    dve.wait_ge(s_rank, j)
                dve.tensor_scalar(msel[:], bank[6][:, 384:384 + E], top[:, j, 1:2], None, ALU.is_ge).then_inc(s_sel, 1)
                dve.max_index(topi[:, j, :], top[:, j, :], bank[6][:, 384:384 + E]).then_inc(s_top, 1)
                dve.wait_ge(s_sel, j + 1)
                if j not in (0, NCH1):
                    dve.wait_ge(s_count, j)
                    dve.tensor_tensor(msum[:, j, :], msum[:, j - 1, :], msel[:], ALU.add).then_inc(s_count, 1)
                else:
                    dve.tensor_copy(msum[:, j, :], msel[:]).then_inc(s_count, 1)

            def place(j):
                dve.wait_ge(s_rank, j + 1)
                dve.wait_ge(s_top, j + 1)
                for k in range(2):
                    mark(dve.scalar_tensor_tensor(rjunk[:, k], iota, topi[:, j, k:k + 1], bank[6][:, 448:448 + E],
                                                  ALU.is_equal, ALU.mult, accum_out=rank[:, k:k + 1]))
                marked()
                slots = float(SLOTS if j < NCH1 else SLOTS2)
                mark(dve.scalar_tensor_tensor(slot[:, j, :], topi[:, j, 0:2], slots, rank[:], ALU.mult, ALU.add))
                mark(dve.tensor_scalar(far[:], rank[:], slots, FAR, ALU.is_ge, ALU.mult))
                marked()
                dve.tensor_tensor(s_idx[:, j, :], slot[:, j, :], far[:], ALU.add).then_inc(s_slot, 1)

            def gather_slots(r, first, last):
                dve.tensor_scalar(g_idx[:, first:last], slot[:, first:last], float(ROWS[r] - 1), None, ALU.min).then_inc(s_gidx, 1)

            mask_pieces(LEAD)
            for c in range(NCH):
                a, b, d = c - 1, c - 2, c - 3
                share = VECTOR_SHARES[len(pool_units(c))]
                mask_pieces(share[0])
                if d >= 0:
                    add_attended(d)
                if b >= 0:
                    stats_qk(b)
                if c == 0:
                    turn_rope()
                mask_pieces(share[1])
                if d >= 0:
                    norm_xf(d)
                if b >= 0:
                    norm_qk(b)
                mask_pieces(share[2])
                if d >= 0:
                    choose(d)
                mask_pieces(share[3])
                if d >= 0:
                    place(d)
                if b >= 0:
                    scores(b)
                mask_pieces(share[4])
                if b >= 0:
                    less_max(b)
                if a >= 0:
                    stats_h(a)
                mask_pieces(share[5])
                if b >= 0:
                    heads(b)
                if a >= 0:
                    norm_h(a)
                if c == 0:
                    dve.wait_ge(s_rem, 32)
                    dve.wait_ge(s_mrem, 16)
                    dve.tensor_tensor(wrem[0:GREM], wrem[0:GREM],
                                      mrem[0:GREM, :].rearrange("p (a n) -> p a n", a=1).to_broadcast([GREM, S, D]),
                                      ALU.mult).then_inc(s_remm, 1)

            def shared_mid(i):
                dve.wait_ge(s_ssil, i + 1)
                dve.tensor_tensor(shs, ssil, bank[1][:], ALU.mult).then_inc(s_shs, 1)

            def add_shared(i):
                dve.wait_ge(s_sh2, i + 1)
                hv = hres[:, 4 * i:4 * i + 4, :].rearrange("p j d -> p (j d)")
                dve.tensor_tensor(hv, hv, bank[5][:], ALU.add).then_inc(s_shared, 1)

            j, k, l = NCH - 3, NCH - 2, NCH - 1
            add_attended(j)
            stats_qk(k)
            norm_xf(j)
            norm_qk(k)
            stats_h(l)
            choose(j)
            norm_h(l)
            place(j)
            gather_slots(0, 0, NCH1)
            scores(k)
            less_max(k)
            stats_qk(l)
            shared_mid(0)
            heads(k)
            norm_qk(l)
            add_attended(k)
            norm_xf(k)
            choose(k)
            place(k)
            add_shared(0)
            scores(l)
            less_max(l)
            heads(l)
            add_attended(l)
            norm_xf(l)
            choose(l)
            place(l)
            gather_slots(1, NCH1, NCH)
            dve.wait_ge(s_total, 1)
            for r in range(2):
                mark(dve.tensor_reduce(flag[:, r:r + 1], bank[6][:, E * r:E * r + E], AX.X, ALU.max))
            marked()
            then(dve.scalar_tensor_tensor(flag[:, 0:1], flag[:, 1:2], float(SLOTS // SLOTS2), flag[:, 0:1], ALU.mult, ALU.max))
            dve.tensor_scalar(flag_i[:], flag[:, 0:1], float(SLOTS), None, ALU.is_gt).then_inc(s_flag, 1)
            def copy_xsT(g):
                dve.wait_ge(s_t1, g + 1)
                dve.wait_ge(s_m1, g - 1)
                dve.tensor_copy(xsT[g % 2], bank[T_BANK(g)][:]).then_inc(s_xsT, 1)

            def mid(g):
                dve.wait_ge(s_sil, g + 1)
                dve.wait_ge(s_t2, g - 1)
                for r in range(4):
                    rows, half = slice(SLOTS2 * r, SLOTS2 * (r + 1)), r % 2 * H
                    last = dve.tensor_tensor(hm[2 + g % 2][rows, :, half:half + H], sil[g % 2][rows],
                                             bank[U_BANK(g)][rows].rearrange("p (i f) -> p i f", f=2 * H)[:, :, H:2 * H], ALU.mult)
                last.then_inc(s_hm, 1)

            def combine(j):
                dve.wait_ge(s_yg[j], 32)
                if j == 0:
                    dve.wait_ge(s_shared, 2)
                then(dve.scalar_tensor_tensor(fin[:, j, :], yg[:, 2 * j, :], wts[:, j, 0:1], hres[:, j, :], ALU.mult, ALU.add))
                dve.scalar_tensor_tensor(fin[:, j, :], yg[:, 2 * j + 1, :], wts[:, j, 1:2], fin[:, j, :],
                                         ALU.mult, ALU.add).then_inc(s_fin, 1)

            dve.wait_ge(s_hmz, 2)
            dve.wait_ge(s_xsT, GROUPS1)
            copy_xsT(GROUPS1)
            copy_xsT(GROUPS1 + 1)
            dve.wait_ge(s_hm, GROUPS1)
            for g in range(GROUPS1, GROUPS):
                mid(g)
                if g + 2 < GROUPS:
                    copy_xsT(g + 2)
            shared_mid(1)
            dve.wait_ge(s_exp, 1)
            then(dve.tensor_scalar(ew[:, 1], ew[:, 0], 1.0, None, ALU.add))
            then(dve.reciprocal(ew[:, 2], ew[:, 1]))
            then(dve.scalar_tensor_tensor(ew[:, 0, :, 0], ew[:, 2, :, 0], 1e-20, ew[:, 2, :, 1], ALU.add, ALU.add))
            then(dve.reciprocal(ew[:, 0, :, 1], ew[:, 0, :, 0]))
            for n in range(2):
                mark(dve.scalar_tensor_tensor(wts[:, :, n], ew[:, 2, :, n], ROUTE_SCALE, ew[:, 0, :, 1], ALU.mult, ALU.mult))
            marked()
            add_shared(1)
            for j in range(NCH):
                combine(j)

            full = dve.value_load(flag_i[0:1, 0:1], min_val=0, max_val=1)
            with dve.If(full == 1):
                dve.wait_ge(s_fm, 16)
                mark(dve.tensor_copy(m_bf, m_in))
                for j in range(NCH):
                    then(dve.tensor_scalar(pick, iota, topi[:, j, 0:1], None, ALU.is_equal))
                    dve.scalar_tensor_tensor(sel_bf[:, j, :], iota, topi[:, j, 1:2], pick, ALU.is_equal, ALU.add).then_inc(s_fsel, 1)
                    dve.wait_ge(s_fsel, j + 1)
                for j in range(NCH):
                    if j >= 1:
                        dve.wait_ge(s_fgate, j)
                    then(dve.scalar_tensor_tensor(pick, iota, topi[:, j, 0:1], wts[:, j, 0:1].to_broadcast([P, E]),
                                                  ALU.is_equal, ALU.mult))
                    mark(dve.scalar_tensor_tensor(gates[:, j, :], iota, topi[:, j, 1:2], wts[:, j, 1:2].to_broadcast([P, E]),
                                                  ALU.is_equal, ALU.mult))
                    marked()
                    then(dve.tensor_tensor(pick, pick, gates[:, j, :], ALU.add))
                    dve.wait_ge(s_fpos, j + 1)
                    dve.scalar_tensor_tensor(gates[:, j, :], bank[6][:, 0:E], float(CAP), pick, ALU.is_lt, ALU.mult).then_inc(s_fgate, 1)
                dve.wait_ge(s_out, 16 * NCH)
                dve.wait_ge(s_fgate, NCH)
                dve.tensor_copy(fin[:], hres[:]).then_inc(s_facc, 1)
                with dve.Fori(0, PAIRS) as i:
                    for j in range(NCH):
                        dve.wait_ge(s_fsil, i * NCH + (j + 1))
                        dve.tensor_tensor(f_mid.rearrange("p (a h) -> p a h", h=H), f_sil,
                                          bank[0][:, 0:4 * H].rearrange("p (a f) -> p a f", a=2)[:, :, H:2 * H],
                                          ALU.mult).then_inc(s_fg, 1)
                        dve.wait_ge(s_fg, i * NCH + (j + 1))
                        gj = gates[:, j, bass.ds(i * 2, 2)].rearrange("p (a b) -> p a b", b=1)
                        dve.tensor_tensor(f_mid.rearrange("p (a h) -> p a h", h=H), f_mid.rearrange("p (a h) -> p a h", h=H),
                                          gj.to_broadcast([P, 2, H]), ALU.mult).then_inc(s_fmid, 1)
                        dve.wait_ge(s_f2, i * NCH + (j + 1))
                        dve.tensor_tensor(fin[:, j, :], fin[:, j, :], bank[2][:, 0:D], ALU.add).then_inc(s_facc, 1)


_INS = ['x', 'L0_tok_weight', 'L0_tok_bias', 'L0_tok_mask', 'L0_attn_W_dq', 'L0_attn_W_uq', 'L0_attn_W_qr', 'L0_attn_W_dkv',
        'L0_attn_W_ukv', 'L0_attn_W_kr', 'L0_attn_W_o', 'L0_attn_q_ln_g', 'L0_attn_q_ln_b', 'L0_attn_kv_ln_g',
        'L0_attn_kv_ln_b', 'L0_ffn_gate_w', 'L0_ffn_w1', 'L0_ffn_w3', 'L0_ffn_w2', 'L0_ffn_sw1', 'L0_ffn_sw3', 'L0_ffn_sw2']
_OUTS = [((B, S, D), 'float32')]


def kernel(**inputs):
    import numpy as _np
    import concourse.bacc as _bacc
    from concourse import mybir as _mybir
    from concourse.bass_utils import run_bass_kernel_spmd as _run

    nc = _bacc.Bacc("TRN2", target_bir_lowering=False, num_devices=1)
    arrays, args = {}, []
    for name in _INS:
        a = _np.ascontiguousarray(inputs[name])
        arrays[f"in_{name}_dram"] = a
        args.append(nc.dram_tensor(f"in_{name}_dram", a.shape, _mybir.dt.from_np(a.dtype), kind="ExternalInput").ap())
    for name, c in (("consts_dram", shape_constants()), ("masks_dram", order_masks())):
        arrays[name] = c
        args.append(nc.dram_tensor(name, c.shape, _mybir.dt.from_np(c.dtype), kind="ExternalInput").ap())
    for i, (shape, dtype) in enumerate(_OUTS):
        dt = _mybir.dt.from_np(_np.dtype(dtype))
        args.append(nc.dram_tensor(f"out_{i}_dram", shape, dt, kind="ExternalOutput").ap())
    tower_kernel(nc, *args)
    r = _run(nc, [arrays], core_ids=[0])
    got = tuple(r.results[0][f"out_{i}_dram"] for i in range(len(_OUTS)))
    return got[0]
```
